# Optimizing a Trainium2 kernel written in Bass

```python
import numpy as np
import jax
import jax.numpy as jnp

def _softmax(x, axis=-1):
    return jax.nn.softmax(x, axis=axis)

def _gelu(x):
    return jax.nn.gelu(x, approximate=True)

def _silu(x):
    return jax.nn.silu(x)

def _sigmoid(x):
    return jax.nn.sigmoid(x)

def _layernorm(x, axis=-1, eps=1e-05):
    m = jnp.mean(x, axis=axis, keepdims=True)
    v = jnp.var(x, axis=axis, keepdims=True)
    return (x - m) / jnp.sqrt(v + eps)

def _scatter_add(tgt, idx, src, axis=0):
    return tgt.at[idx].add(src)

def _segment_sum(src, seg, n):
    return jax.ops.segment_sum(src, seg, n)
kernel_name = 'mk_dlrm_tower_d1_rec_r8_31212e'

def setup_inputs(seed: int=0):
    np.random.seed(seed)
    _w = jnp.asarray

    def _rec_inputs():
        import jax
        import jax.numpy as jnp
        _tk = jax.random.key(seed)
        ids = jnp.stack([jax.random.randint(jax.random.fold_in(_tk, 200 + f), (512,), 0, v, jnp.int32) for f, v in enumerate([125000, 125000, 12500, 12500, 125000, 12500, 12500, 1000, 12500, 1250, 12500, 1000, 12500, 1000, 1250, 1250, 1250, 12500, 1250, 1000, 1250, 1000, 1000, 1250, 1000, 1250])], axis=1)
        tbl_0 = 0.05 * jax.random.normal(jax.random.fold_in(_tk, 500 + 0), (125000, 64), jnp.float32)
        tbl_1 = 0.05 * jax.random.normal(jax.random.fold_in(_tk, 500 + 1), (125000, 64), jnp.float32)
        tbl_2 = 0.05 * jax.random.normal(jax.random.fold_in(_tk, 500 + 2), (12500, 64), jnp.float32)
        tbl_3 = 0.05 * jax.random.normal(jax.random.fold_in(_tk, 500 + 3), (12500, 64), jnp.float32)
        tbl_4 = 0.05 * jax.random.normal(jax.random.fold_in(_tk, 500 + 4), (125000, 64), jnp.float32)
        tbl_5 = 0.05 * jax.random.normal(jax.random.fold_in(_tk, 500 + 5), (12500, 64), jnp.float32)
        tbl_6 = 0.05 * jax.random.normal(jax.random.fold_in(_tk, 500 + 6), (12500, 64), jnp.float32)
        tbl_7 = 0.05 * jax.random.normal(jax.random.fold_in(_tk, 500 + 7), (1000, 64), jnp.float32)
        tbl_8 = 0.05 * jax.random.normal(jax.random.fold_in(_tk, 500 + 8), (12500, 64), jnp.float32)
        tbl_9 = 0.05 * jax.random.normal(jax.random.fold_in(_tk, 500 + 9), (1250, 64), jnp.float32)
        tbl_10 = 0.05 * jax.random.normal(jax.random.fold_in(_tk, 500 + 10), (12500, 64), jnp.float32)
        tbl_11 = 0.05 * jax.random.normal(jax.random.fold_in(_tk, 500 + 11), (1000, 64), jnp.float32)
        tbl_12 = 0.05 * jax.random.normal(jax.random.fold_in(_tk, 500 + 12), (12500, 64), jnp.float32)
        tbl_13 = 0.05 * jax.random.normal(jax.random.fold_in(_tk, 500 + 13), (1000, 64), jnp.float32)
        tbl_14 = 0.05 * jax.random.normal(jax.random.fold_in(_tk, 500 + 14), (1250, 64), jnp.float32)
        tbl_15 = 0.05 * jax.random.normal(jax.random.fold_in(_tk, 500 + 15), (1250, 64), jnp.float32)
        tbl_16 = 0.05 * jax.random.normal(jax.random.fold_in(_tk, 500 + 16), (1250, 64), jnp.float32)
        tbl_17 = 0.05 * jax.random.normal(jax.random.fold_in(_tk, 500 + 17), (12500, 64), jnp.float32)
        tbl_18 = 0.05 * jax.random.normal(jax.random.fold_in(_tk, 500 + 18), (1250, 64), jnp.float32)
        tbl_19 = 0.05 * jax.random.normal(jax.random.fold_in(_tk, 500 + 19), (1000, 64), jnp.float32)
        tbl_20 = 0.05 * jax.random.normal(jax.random.fold_in(_tk, 500 + 20), (1250, 64), jnp.float32)
        tbl_21 = 0.05 * jax.random.normal(jax.random.fold_in(_tk, 500 + 21), (1000, 64), jnp.float32)
        tbl_22 = 0.05 * jax.random.normal(jax.random.fold_in(_tk, 500 + 22), (1000, 64), jnp.float32)
        tbl_23 = 0.05 * jax.random.normal(jax.random.fold_in(_tk, 500 + 23), (1250, 64), jnp.float32)
        tbl_24 = 0.05 * jax.random.normal(jax.random.fold_in(_tk, 500 + 24), (1000, 64), jnp.float32)
        tbl_25 = 0.05 * jax.random.normal(jax.random.fold_in(_tk, 500 + 25), (1250, 64), jnp.float32)
        _rk = jax.random.fold_in(_tk, 7)
        r_dense_t = 7.22013e-05 + 1.00017 * jax.random.normal(jax.random.fold_in(_rk, 101), (512, 256), jnp.float32)
        W_top1 = 0.0360844 * jax.random.normal(jax.random.fold_in(_tk, 801), (768, 512), jnp.float32)
        W_top2 = 0.0441942 * jax.random.normal(jax.random.fold_in(_tk, 802), (512, 256), jnp.float32)
        W_top3 = 0.0625 * jax.random.normal(jax.random.fold_in(_tk, 803), (256, 1), jnp.float32)
        b_top1 = jnp.zeros((512,), jnp.float32)
        b_top2 = jnp.zeros((256,), jnp.float32)
        return (r_dense_t, ids, tbl_0, tbl_1, tbl_2, tbl_3, tbl_4, tbl_5, tbl_6, tbl_7, tbl_8, tbl_9, tbl_10, tbl_11, tbl_12, tbl_13, tbl_14, tbl_15, tbl_16, tbl_17, tbl_18, tbl_19, tbl_20, tbl_21, tbl_22, tbl_23, tbl_24, tbl_25, W_top1, b_top1, W_top2, b_top2, W_top3)
    r_dense_t, ids, tbl_0, tbl_1, tbl_2, tbl_3, tbl_4, tbl_5, tbl_6, tbl_7, tbl_8, tbl_9, tbl_10, tbl_11, tbl_12, tbl_13, tbl_14, tbl_15, tbl_16, tbl_17, tbl_18, tbl_19, tbl_20, tbl_21, tbl_22, tbl_23, tbl_24, tbl_25, W_top1, b_top1, W_top2, b_top2, W_top3 = _rec_inputs()

    def _L0_rec_setup():
        import jax, jax.numpy as jnp
        import numpy as np
        EPS = 1e-05
        NI = 33
        TRIL_I, TRIL_J = np.tril_indices(NI, k=-1)

        def layer_norm(x, g, b):
            m = jnp.mean(x, axis=-1, keepdims=True)
            v = jnp.mean(jnp.square(x - m), axis=-1, keepdims=True)
            return (x - m) * jax.lax.rsqrt(v + EPS) * g + b
        key = jax.random.key(seed)
        ks = jax.random.split(key, 8)
        B, D_DENSE, N_SP, D_SP = (4096, 256, 26, 64)
        E, PROJ, MAXD, NFLAT = (128, 32, 512, 528)
        dense_t = jax.random.normal(ks[0], (B, D_DENSE), dtype=jnp.float32)
        sparse_t = jax.random.normal(ks[1], (B, N_SP, D_SP), dtype=jnp.float32)
        Wd = jax.random.normal(ks[2], (E, D_DENSE), dtype=jnp.float32) / np.sqrt(D_DENSE)
        Ws = jax.random.normal(ks[3], (E, D_SP), dtype=jnp.float32) / np.sqrt(D_SP)
        Wsi = jax.random.normal(ks[4], (PROJ, N_SP), dtype=jnp.float32) / np.sqrt(N_SP)
        Wl = jax.random.normal(ks[5], (MAXD, NFLAT), dtype=jnp.float32) / np.sqrt(NFLAT)
        gd = jnp.ones((E,), jnp.float32)
        bd = jnp.zeros((E,), jnp.float32)
        gs = jnp.ones((E,), jnp.float32)
        bs = jnp.zeros((E,), jnp.float32)
        gsi = jnp.ones((PROJ,), jnp.float32)
        bsi = jnp.zeros((PROJ,), jnp.float32)
        gl = jnp.ones((MAXD,), jnp.float32)
        bl = jnp.zeros((MAXD,), jnp.float32)
        return {'dense_t': dense_t, 'sparse_t': sparse_t, 'Wd': Wd, 'gd': gd, 'bd': bd, 'Ws': Ws, 'gs': gs, 'bs': bs, 'Wsi': Wsi, 'gsi': gsi, 'bsi': bsi, 'Wl': Wl, 'gl': gl, 'bl': bl, 'dims_in_use': 384}
    _L0_rec_all = _L0_rec_setup()
    _L0_rec_in = {k: v for k, v in _L0_rec_all.items() if k in ('Wd', 'gd', 'bd', 'Ws', 'gs', 'bs', 'Wsi', 'gsi', 'bsi', 'Wl', 'gl', 'bl')}
    del _L0_rec_all
    return {'r_dense_t': r_dense_t, 'ids': ids, 'tbl_0': tbl_0, 'tbl_1': tbl_1, 'tbl_2': tbl_2, 'tbl_3': tbl_3, 'tbl_4': tbl_4, 'tbl_5': tbl_5, 'tbl_6': tbl_6, 'tbl_7': tbl_7, 'tbl_8': tbl_8, 'tbl_9': tbl_9, 'tbl_10': tbl_10, 'tbl_11': tbl_11, 'tbl_12': tbl_12, 'tbl_13': tbl_13, 'tbl_14': tbl_14, 'tbl_15': tbl_15, 'tbl_16': tbl_16, 'tbl_17': tbl_17, 'tbl_18': tbl_18, 'tbl_19': tbl_19, 'tbl_20': tbl_20, 'tbl_21': tbl_21, 'tbl_22': tbl_22, 'tbl_23': tbl_23, 'tbl_24': tbl_24, 'tbl_25': tbl_25, 'W_top1': W_top1, 'b_top1': b_top1, 'W_top2': W_top2, 'b_top2': b_top2, 'W_top3': W_top3, 'L0_rec_Wd': _L0_rec_in['Wd'], 'L0_rec_gd': _L0_rec_in['gd'], 'L0_rec_bd': _L0_rec_in['bd'], 'L0_rec_Ws': _L0_rec_in['Ws'], 'L0_rec_gs': _L0_rec_in['gs'], 'L0_rec_bs': _L0_rec_in['bs'], 'L0_rec_Wsi': _L0_rec_in['Wsi'], 'L0_rec_gsi': _L0_rec_in['gsi'], 'L0_rec_bsi': _L0_rec_in['bsi'], 'L0_rec_Wl': _L0_rec_in['Wl'], 'L0_rec_gl': _L0_rec_in['gl'], 'L0_rec_bl': _L0_rec_in['bl']}

def reference(r_dense_t, ids, tbl_0, tbl_1, tbl_2, tbl_3, tbl_4, tbl_5, tbl_6, tbl_7, tbl_8, tbl_9, tbl_10, tbl_11, tbl_12, tbl_13, tbl_14, tbl_15, tbl_16, tbl_17, tbl_18, tbl_19, tbl_20, tbl_21, tbl_22, tbl_23, tbl_24, tbl_25, W_top1, b_top1, W_top2, b_top2, W_top3, L0_rec_Wd, L0_rec_gd, L0_rec_bd, L0_rec_Ws, L0_rec_gs, L0_rec_bs, L0_rec_Wsi, L0_rec_gsi, L0_rec_bsi, L0_rec_Wl, L0_rec_gl, L0_rec_bl):
    import jax
    import jax.numpy as jnp

    def _L0_rec_ref(dense_t, sparse_t, Wd, gd, bd, Ws, gs, bs, Wsi, gsi, bsi, Wl, gl, bl, dims_in_use):
        import jax, jax.numpy as jnp
        import numpy as np
        EPS = 1e-05
        NI = 33
        TRIL_I, TRIL_J = np.tril_indices(NI, k=-1)

        def layer_norm(x, g, b):
            m = jnp.mean(x, axis=-1, keepdims=True)
            v = jnp.mean(jnp.square(x - m), axis=-1, keepdims=True)
            return (x - m) * jax.lax.rsqrt(v + EPS) * g + b
        x = layer_norm(dense_t @ Wd.T, gd, bd)
        y = layer_norm(jnp.einsum('bnd,ed->bne', sparse_t, Ws), gs, bs)
        y = jnp.einsum('bne,pn->bep', y, Wsi)
        y = layer_norm(y, gsi, bsi)
        y = jnp.swapaxes(y, 1, 2)
        T = jnp.concatenate([x[:, None, :], y], axis=1)
        Z = jnp.einsum('bnd,bmd->bnm', T, T)
        Zflat = Z[:, TRIL_I, TRIL_J]
        out = layer_norm(Zflat @ Wl.T, gl, bl)
        maxd = out.shape[-1]
        mask = (jnp.arange(maxd) < dims_in_use).astype(out.dtype)
        return out * mask
    e = jnp.stack([tbl_0[ids[:, 0]], tbl_1[ids[:, 1]], tbl_2[ids[:, 2]], tbl_3[ids[:, 3]], tbl_4[ids[:, 4]], tbl_5[ids[:, 5]], tbl_6[ids[:, 6]], tbl_7[ids[:, 7]], tbl_8[ids[:, 8]], tbl_9[ids[:, 9]], tbl_10[ids[:, 10]], tbl_11[ids[:, 11]], tbl_12[ids[:, 12]], tbl_13[ids[:, 13]], tbl_14[ids[:, 14]], tbl_15[ids[:, 15]], tbl_16[ids[:, 16]], tbl_17[ids[:, 17]], tbl_18[ids[:, 18]], tbl_19[ids[:, 19]], tbl_20[ids[:, 20]], tbl_21[ids[:, 21]], tbl_22[ids[:, 22]], tbl_23[ids[:, 23]], tbl_24[ids[:, 24]], tbl_25[ids[:, 25]]], axis=1)
    z = _L0_rec_ref(r_dense_t, e, L0_rec_Wd, L0_rec_gd, L0_rec_bd, L0_rec_Ws, L0_rec_gs, L0_rec_bs, L0_rec_Wsi, L0_rec_gsi, L0_rec_bsi, L0_rec_Wl, L0_rec_gl, L0_rec_bl, 384)
    z = z.reshape(z.shape[0], -1)
    h = jnp.concatenate([z, r_dense_t], axis=1)
    h = jnp.maximum(h @ W_top1 + b_top1, 0.0)
    h = jnp.maximum(h @ W_top2 + b_top2, 0.0)
    y = h @ W_top3
    return y

_drawn_inputs = setup_inputs


def setup_inputs(seed=0):
    import zlib

    import numpy as np

    out = dict(_drawn_inputs(seed))
    spreads = {'b_top1': (0.0, 0.1),
     'b_top2': (0.0, 0.1),
     'L0_rec_gd': (1.0, 0.6),
     'L0_rec_bd': (0.0, 0.8),
     'L0_rec_gs': (1.0, 0.6),
     'L0_rec_bs': (0.0, 0.1),
     'L0_rec_gsi': (1.0, 0.2),
     'L0_rec_bsi': (0.0, 0.1),
     'L0_rec_gl': (1.0, 0.2),
     'L0_rec_bl': (0.0, 0.1)}
    factors = {}
    for name, (base, spread) in spreads.items():
        noise = np.random.default_rng([zlib.crc32(name.encode()), seed]).standard_normal(out[name].shape)
        drawn = base * np.exp(spread * noise) if base else spread * noise
        out[name] = jnp.asarray(drawn.astype(out[name].dtype))
    for name, factor in factors.items():
        out[name] = (out[name] * factor).astype(out[name].dtype)
    return out
```

```python
from contextlib import ExitStack

import concourse.bass as bass
import numpy as np
from concourse import mybir

F32 = mybir.dt.float32
F32R = mybir.dt.float32r
U32 = mybir.dt.uint32
ALU = mybir.AluOpType
ACT = mybir.ActivationFunctionType
AX = mybir.AxisListType

P = 128
B, N_TBL, D, E, PROJ = 512, 26, 64, 128, 32
VOCAB = [125000, 125000, 12500, 12500, 125000, 12500, 12500, 1000, 12500, 1250, 12500, 1000, 12500,
         1000, 1250, 1250, 1250, 12500, 1250, 1000, 1250, 1000, 1000, 1250, 1000, 1250]
MAXD, USED, D_DENSE = 512, 384, 256
H1, H2 = 512, 256
EPS = 1e-5

CHUNK = 64
NC = B // CHUNK
TILES = CHUNK * N_TBL // P
WIN = 16
NW = CHUNK // WIN
NG = WIN // 4
BLK = 128
NK = B // BLK
TOUCH = 6
C = PROJ + 2
WRAP = PROJ // 2
ROW = PROJ + WRAP
FEAT5 = ROW + PROJ
ONE = PROJ + 1
NQ = 4
QT = PROJ // NQ
PAIRS = [[0, 1], [2, 3], [4], [5, 6]]
NPAIR = 7
NBUF = 4
GROUP = [(0, 8), (8, TILES)]


SHIFT_ROWS = slice(D, D + 3)


def first_sample(t):
    return P * t // N_TBL


def pieces(w):
    out = []
    for t in range(TILES):
        lo, hi = first_sample(t), (P * t + P - 1) // N_TBL + 1
        a, b = max(lo, WIN * w), min(hi, WIN * (w + 1))
        if a < b:
            out.append((t, a - WIN * w, b - a, a - lo))
    return out


def tower(nc, tables, ids, base, consts, wst, wsi_rows, gs, bs, gsi_pairs, gsi, bsi, wlt, wlx,
          dense_t, wdt, gd, bd, gl, bl, w1, b1, w2, b2, w3, out):
    ctx = ExitStack()
    with ctx:
        def sb(name, shape, dt=F32):
            return ctx.enter_context(nc.sbuf_tensor(name, shape, dt))

        def sem(name):
            return ctx.enter_context(nc.semaphore(name))

        ids_sb = sb("ids_sb", [P, NC * TILES], U32)
        base_sb = sb("base_sb", [P, NC * TILES], U32)
        idx = sb("idx", [P, NC * TILES], U32)
        NCONST = P + TILES * TOUCH + 2 * NQ * FEAT5 + 4
        const_sb = sb("const_sb", [P, NCONST])
        ident = const_sb[:, 0:P]
        mask = const_sb[:, P:P + TILES * TOUCH].rearrange("p (t b) -> p t b", t=TILES)
        hot_at = P + TILES * TOUCH
        hot_q = const_sb[:, hot_at:hot_at + NQ * FEAT5].rearrange("p (i c) -> p i c", i=NQ)
        hot_p = const_sb[:, hot_at + NQ * FEAT5:NCONST - 4].rearrange("p (i c) -> p i c", i=NQ)
        pick = const_sb[SHIFT_ROWS, NCONST - 4:NCONST]
        wst_sb = sb("wst_sb", [P, E])
        wc = sb("wc", [P, E])
        wce = sb("wce", [E, P])
        gram = sb("gram", [P, 2 * D])
        gs_sb = sb("gs_sb", [P, E])
        wg = sb("wg", [P, E])
        wg_hi = sb("wg_hi", [P, E], F32R)
        wg_lo = sb("wg_lo", [P, E], F32R)
        wg_bs = sb("wg_bs", [D + 3, E], F32R)
        bs_sb = sb("bs_sb", [D + 3, 4, E])
        bs_hi = sb("bs_hi", [D + 3, E], F32R)
        sw = sb("sw", [D + 3, 4, PROJ])
        sw_hi = sb("sw_hi", [D + 3, PROJ], F32R)
        wsi_sb = sb("wsi_sb", [P, TILES, PROJ])
        wsic = sb("wsic", [P, TILES, PROJ])
        wsi_hi = sb("wsi_hi", [P, TILES, PROJ], F32R)
        wsi_lo = sb("wsi_lo", [P, TILES, PROJ])
        mix_hi = sb("mix_hi", [P, TILES, TOUCH, PROJ], F32R)
        mix_lo = sb("mix_lo", [P, TILES, TOUCH, PROJ], F32R)
        pp_sb = sb("pp_sb", [P, 4, NQ])
        cf = sb("cf", [P, 4, NQ])
        gsi_sb = sb("gsi_sb", [PROJ, 1])
        bsi_sb = sb("bsi_sb", [PROJ, 1])
        wl_sb = sb("wl_sb", [P, NQ, MAXD])
        wlc = sb("wlc", [P, NQ, MAXD])
        wlm = sb("wlm", [P, NQ, MAXD])
        wlx_sb = sb("wlx_sb", [PROJ, MAXD])
        wlxc = sb("wlxc", [PROJ, MAXD])
        mm = sb("mm", [P, NQ, FEAT5])
        mmx = sb("mmx", [PROJ, FEAT5])
        mt = sb("mt", [P, NQ, FEAT5])
        wl5 = sb("wl5", [FEAT5, MAXD])
        dn = sb("dn", [P, 2, B])
        wd_sb = sb("wd_sb", [P, 2, E])
        wdc = sb("wdc", [P, 2, E])
        vec = sb("vec", [P, 2 + 3 + 3 + 4 + 2 + 2])
        gd_c, bd_c = vec[:, 0:1], vec[:, 1:2]
        gl_c, bl_c = vec[:, 2:5], vec[:, 5:8]
        b1_c, b2_c, w3_c = vec[:, 8:12], vec[:, 12:14], vec[:, 14:16]
        w1_sb = sb("w1_sb", [P, 5, H1])
        w2_sb = sb("w2_sb", [P, 4, H2])
        sums = sb("sums", [P, 64])
        ones_e = sb("ones_e", [P, P])
        ones_1 = sb("ones_1", [P, P])
        eps = sb("eps", [P, 1])
        lsum = sb("lsum", [P, 10])
        xsq = sb("xsq", [P, B])
        xsd = sb("xsd", [P, B])
        xr = sb("xr", [P, B])
        xn = sb("xn", [P, B])
        xt = sb("xt", [P, B])
        sumx = sb("sumx", [P, NK])

        emb = sb("emb", [P, NBUF, TILES, D])
        et = sb("et", [P, NPAIR, P])
        qe = sb("qe", [P, 8, D])
        var = sb("var", [P, TILES])
        std = sb("std", [P, TILES])
        rstd = sb("rstd", [P, TILES])
        es = sb("es", [P, 2, TILES, D])
        es2 = sb("es2", [P, 2, TILES, 2, D], F32R)
        u1 = sb("u1", [P, 2, WIN * PROJ], F32R)
        u2 = sb("u2", [D + 3, 2, WIN * PROJ], F32R)
        vsq = sb("vsq", [P, 2, WIN * PROJ])
        ss = sb("ss", [P, 2, WIN])
        sd = sb("sd", [P, 2, WIN])
        r2 = sb("r2", [P, 2, WIN])
        T = sb("T", [P, 2, CHUNK, C])
        zs = sb("zs", [P, BLK // 4, C])
        ZT = sb("ZT", [P, ROW * (C + 1)])
        zt = ZT[:, 0:ROW * C].rearrange("p (c q) -> p c q", c=C)
        zp = sb("zp", [P, PROJ, WRAP])
        zf = sb("zf", [P, NQ + 1, BLK])
        osq = sb("osq", [P, MAXD])
        ost = sb("ost", [P, 3])
        on = sb("on", [P, USED])
        zn = sb("zn", [P, 3, BLK])
        h1d = sb("h1d", [P, 4, B])
        h1s = sb("h1s", [P, 4, BLK])
        h1 = sb("h1", [P, 4, BLK])
        h2 = sb("h2", [P, 2, BLK])
        y_sb = sb("y_sb", [1, B])

        ps = ctx.enter_context(nc.psum_tensor("ps", [P, 8, 512], F32))
        etp = ps[:, 0, :].rearrange("p (u r) -> p u r", u=4)
        qp = ps[:, 1, :].rearrange("p (t d) -> p t d", d=D)
        up = [ps[:, 2, :], ps[:, 3, :]]
        vp = [ps[:, 4, :], ps[:, 5, :]]
        gp = ps[:, 6, :]
        fp = ps[:, 7, :]
        hd_bank = [up[0], up[1], gp, fp]
        GPW = NG * C

        ld_ids, ld_const, ld_ws, ld_wsi, ld_x, ld_dense, ld_vec, ld_wl, ld_top = [
            sem(n) for n in ("ld_ids", "ld_const", "ld_ws", "ld_wsi", "ld_x", "ld_dense", "ld_vec", "ld_wl", "ld_top")]
        gath = [[sem(f"gath{a}_{i}") for i in range(NPAIR)] for a in range(NBUF)]
        prep = sem("prep")
        idx_ok, wc_ok, mix_ok, wd_ok, fill_ok, m_ok = [
            sem(n) for n in ("idx_ok", "wc_ok", "mix_ok", "wd_ok", "fill_ok", "m_ok")]
        p_wce, p_gram, p_sw, p_x, p_xv, p_s, p_w5 = [
            sem(n) for n in ("p_wce", "p_gram", "p_sw", "p_x", "p_xv", "p_s", "p_w5")]
        a_wce, a_gram, a_sw, a_xsq, a_xsd, a_s, a_w5 = [
            sem(n) for n in ("a_wce", "a_gram", "a_sw", "a_xsq", "a_xsd", "a_s", "a_w5")]
        xt_ok, cf_ok, wlc_ok, wl_ok, es_hi_ok, es2_ok, u2_ok = [
            sem(n) for n in ("xt_ok", "cf_ok", "wlc_ok", "wl_ok", "es_hi_ok", "es2_ok", "u2_ok")]
        et_t, et_c, q_done, qe_done, var_ok, std_ok, rstd_ok, es_ok = [
            sem(n) for n in ("et_t", "et_c", "q_done", "qe_done", "var_ok", "std_ok", "rstd_ok", "es_ok")]
        u_done, u_copied, v_done, sq_ok, ss_ok, sd_ok, r2_ok, t_ok = [
            sem(n) for n in ("u_done", "u_copied", "v_done", "sq_ok", "ss_ok", "sd_ok", "r2_ok", "t_ok")]
        x_in, g_done, g_copied, zt_ok, zw_ok, f_t, f_c, f5_t, f5_ok = [
            sem(n) for n in ("x_in", "g_done", "g_copied", "zt_ok", "zw_ok", "f_t", "f_c", "f5_t", "f5_ok")]
        o_done, o_ss, o_sd, o_r, on_ok, z_t, z_c = [
            sem(n) for n in ("o_done", "o_ss", "o_sd", "o_r", "on_ok", "z_t", "z_c")]
        hd_done, hd_ok, m1_done, hs_ok, h1_ok, m2_done, h2_ok, m3_done, y_ok, out_ok = [
            sem(n) for n in ("hd_done", "hd_ok", "m1_done", "hs_ok", "h1_ok", "m2_done", "h2_ok", "m3_done", "y_ok", "out_ok")]

        LC = 5
        LV, LG = LC + 1, LC + 3
        SLOTS = NC * NW + LG + 11
        WL_SLOTS = [4, 5, 6, 8, 10]
        W5_SLOT = 12
        N = NC * NW

        def block_at(n, d):
            k, r = divmod(n - d - (2 * NW + LG), 2 * NW)
            return k if r == 0 and 0 <= k < NK else None

        block = ctx.enter_context(nc.Block())

        @block.sync
        def _(sp):
            sp.dma_start(ids_sb[:, :], ids).then_inc(ld_ids, 16)
            sp.dma_start(base_sb[:, :], base).then_inc(ld_ids, 16)
            sp.dma_start(wst_sb[:, :], wst).then_inc(ld_ws, 16)
            sp.dma_start(const_sb[:, :], consts).then_inc(ld_const, 16)
            sp.dma_start(gs_sb[:, :], gs.broadcast_to([P, E])).then_inc(ld_ws, 16)
            sp.dma_start(bs_sb[SHIFT_ROWS, 0, :], bs.broadcast_to([3, E])).then_inc(ld_ws, 16)
            sp.dma_start(wsi_sb[:, :, :], wsi_rows).then_inc(ld_wsi, 16)
            sp.dma_start(wd_sb[:, :, :], wdt).then_inc(ld_x, 16)
            sp.dma_start(dn[:, :, :], dense_t).then_inc(ld_x, 16)
            sp.dma_start(w1_sb[:, 3:5, :], w1[:, 3:5, :]).then_inc(ld_dense, 16)
            sp.dma_start(b1_c, b1).then_inc(ld_dense, 16)
            sp.dma_start(gd_c, gd).then_inc(ld_vec, 16)
            sp.dma_start(bd_c, bd).then_inc(ld_vec, 16)
            sp.dma_start(wl_sb[:, :, :], wlt).then_inc(ld_wl, 16)
            sp.dma_start(wlx_sb[:, :], wlx).then_inc(ld_wl, 16)
            sp.dma_start(pp_sb[:, :, :], gsi_pairs).then_inc(ld_wl, 16)
            sp.dma_start(gsi_sb[:, :], gsi).then_inc(ld_wl, 16)
            sp.dma_start(bsi_sb[:, :], bsi).then_inc(ld_wl, 16)
            sp.dma_start(gl_c, gl).then_inc(ld_top, 16)
            sp.dma_start(bl_c, bl).then_inc(ld_top, 16)
            sp.dma_start(b2_c, b2).then_inc(ld_top, 16)
            sp.dma_start(w3_c, w3).then_inc(ld_top, 16)
            sp.dma_start(w1_sb[:, 0:3, :], w1[:, 0:3, :]).then_inc(ld_top, 16)
            sp.dma_start(w2_sb[:, :, :], w2).then_inc(ld_top, 16)
            sp.wait_ge(y_ok, NK)
            sp.dma_start(out, y_sb[:, :]).then_inc(out_ok, 16)
            sp.wait_ge(out_ok, 16)

        @block.gpsimd
        def _(pool):
            pool.wait_ge(idx_ok, 1)
            for c in range(NC):
                if c >= NBUF:
                    pool.wait_ge(es_ok, 2 * (c - NBUF + 1))
                for t in range(TILES):
                    at = c * TILES + t
                    nc.gpsimd.indirect_dma_start(
                        emb[:, c % NBUF, t, :], None, tables,
                        bass.IndirectOffsetOnAxis(ap=idx[:, at:at + 1], axis=0),
                    ).then_inc(gath[c % NBUF][t // 2], 16)

        @block.vector
        def _(dve):
            step = [0]

            def link(ins):
                step[0] += 1
                ins.then_inc(prep, 1)
                dve.wait_ge(prep, step[0])

            def centre(dst, src, total, shape, n):
                link(nc.vector.tensor_reduce(total, src, AX.X, ALU.add))
                link(nc.vector.scalar_tensor_tensor(
                    out=dst, in0=total.unsqueeze(len(shape) - 1).broadcast_to(shape), scalar=-1.0 / n,
                    in1=src, op0=ALU.mult, op1=ALU.add))

            dve.wait_ge(ld_ids, 32)
            nc.vector.tensor_tensor(idx[:, :], ids_sb[:, :], base_sb[:, :], ALU.add).then_inc(idx_ok, 1)
            nc.vector.memset(ones_e[:, :], 1.0 / E).then_inc(fill_ok, 1)
            nc.vector.memset(ones_1[:, :], 1.0).then_inc(fill_ok, 1)
            nc.vector.memset(eps[:, :], EPS).then_inc(fill_ok, 1)
            nc.vector.memset(T[:, :, :, 1:2], 1.0).then_inc(fill_ok, 1)
            nc.vector.memset(gram[:, :], 0.0).then_inc(fill_ok, 1)
            nc.vector.memset(ZT[:, 0:2 * ROW], 0.0).then_inc(fill_ok, 1)
            dve.wait_ge(fill_ok, 6)
            nc.vector.memset(ZT[:, ONE:ONE + 1], 1.0).then_inc(fill_ok, 1)
            dve.wait_ge(ld_ws, 48)
            link(nc.vector.tensor_reduce(sums[:, 0:1], wst_sb[:, :], AX.X, ALU.add))
            link(nc.vector.tensor_scalar(sums[:, 1:2], sums[:, 0:1], 1.0 / E, None, ALU.mult))
            nc.vector.tensor_scalar(wc[:, :], wst_sb[:, :], sums[:, 1:2], None, ALU.subtract).then_inc(wc_ok, 1)
            dve.wait_ge(ld_wsi, 16)
            dve.wait_ge(ld_const, 16)
            centre(wsic[:, :, :], wsi_sb[:, :, :], sums[:, 2:2 + TILES], [P, TILES, PROJ], PROJ)
            nc.vector.nop().then_inc(mix_ok, 1)
            dve.wait_ge(ld_x, 32)
            centre(wdc[:, :, :], wd_sb[:, :, :], sums[:, 16:18], [P, 2, E], E)
            nc.vector.nop().then_inc(wd_ok, 1)
            link(nc.vector.tensor_copy(wsi_hi[:, :, :], wsic[:, :, :]))
            link(nc.vector.tensor_tensor(wsi_lo[:, :, :], wsic[:, :, :], wsi_hi[:, :, :].bitcast(F32), ALU.subtract))
            for part, whole in ((mix_hi, wsi_hi[:, :, :].bitcast(F32)), (mix_lo, wsi_lo[:, :, :])):
                nc.vector.tensor_tensor(
                    part[:, :, :, :], whole.unsqueeze(2).broadcast_to([P, TILES, TOUCH, PROJ]),
                    mask.unsqueeze(3).broadcast_to([P, TILES, TOUCH, PROJ]), ALU.mult).then_inc(mix_ok, 1)
            dve.wait_ge(wc_ok, 1)
            link(nc.vector.tensor_tensor(wg[:, :], wc[:, :], gs_sb[:, :], ALU.mult))
            link(nc.vector.tensor_copy(wg_hi[:, :], wg[:, :]))
            nc.vector.tensor_copy(wg_bs[0:D, :], wg[0:D, :]).then_inc(wc_ok, 1)
            nc.vector.tensor_tensor(wg_lo[:, :], wg[:, :], wg_hi[:, :].bitcast(F32), ALU.subtract).then_inc(wc_ok, 1)

            def three_rows(dst, parts, hi, a):
                link(nc.vector.tensor_copy(hi[SHIFT_ROWS, :], parts[SHIFT_ROWS, 0, :]))
                link(nc.vector.tensor_tensor(parts[SHIFT_ROWS, 1, :], parts[SHIFT_ROWS, 0, :],
                                             hi[SHIFT_ROWS, :].bitcast(F32), ALU.subtract))
                link(nc.vector.tensor_scalar(parts[SHIFT_ROWS, 2, :], parts[SHIFT_ROWS, 1, :], pick[:, a + 1:a + 2],
                                             None, ALU.mult))
                link(nc.vector.scalar_tensor_tensor(
                    out=dst, in0=hi[SHIFT_ROWS, :].bitcast(F32), scalar=pick[:, a:a + 1],
                    in1=parts[SHIFT_ROWS, 2, :], op0=ALU.mult, op1=ALU.add))

            three_rows(wg_bs[SHIFT_ROWS, :], bs_sb, bs_hi, 0)
            dve.wait_ge(a_sw, 1)
            three_rows(sw[SHIFT_ROWS, 3, :], sw, sw_hi, 2)
            nc.vector.tensor_copy(
                u2[SHIFT_ROWS, :, :].rearrange("p a (s q) -> p (a s) q", q=PROJ),
                sw[SHIFT_ROWS, 3, :].unsqueeze(1).broadcast_to([3, 2 * WIN, PROJ])).then_inc(wc_ok, 1)
            def finish_x():
                dve.wait_ge(ld_vec, 32)
                dve.wait_ge(a_xsd, 1)
                link(nc.vector.reciprocal(xr[:, :], xsd[:, :]))
                link(nc.vector.tensor_tensor(xn[:, :], vp[0], xr[:, :], ALU.mult))
                nc.vector.tensor_scalar(xt[:, :], xn[:, :], gd_c, bd_c, ALU.mult, ALU.add).then_inc(xt_ok, 1)

            def pair_coefficients():
                dve.wait_ge(ld_wl, 80)
                gq, gpr, bq, bp = (pp_sb[:, i, :] for i in range(4))
                nc.vector.tensor_tensor(cf[:, 0, :], gq, gpr, ALU.mult).then_inc(cf_ok, 1)
                link(nc.vector.tensor_tensor(cf[:, 1, :], gq, bp, ALU.mult))
                link(nc.vector.tensor_tensor(cf[:, 2, :], gpr, bq, ALU.mult))
                link(nc.vector.scalar_tensor_tensor(out=cf[:, 3, :], in0=bq, scalar=float(E), in1=bp,
                                                    op0=ALU.mult, op1=ALU.mult))
                link(nc.vector.tensor_tensor(
                    mt[:, :, :], hot_q, cf[:, 1, :].unsqueeze(2).broadcast_to([P, NQ, FEAT5]), ALU.mult))
                link(nc.vector.tensor_tensor(
                    mm[:, :, :], hot_p, cf[:, 2, :].unsqueeze(2).broadcast_to([P, NQ, FEAT5]), ALU.mult))
                link(nc.vector.tensor_tensor(mm[:, :, :], mm[:, :, :], mt[:, :, :], ALU.add))
                link(nc.vector.tensor_copy(mm[:, :, ONE], cf[:, 3, :]))
                link(nc.vector.tensor_scalar(mmx[:, :], const_sb[0:PROJ, 0:FEAT5], gsi_sb[:, :], None, ALU.mult))
                nc.vector.tensor_copy(mmx[:, PROJ:PROJ + 1], bsi_sb[:, :]).then_inc(m_ok, 1)

            def row_statistics(c, a):
                t0, t1 = GROUP[a]
                g = 2 * c + a + 1
                dve.wait_ge(q_done, g)
                nc.vector.tensor_tensor(qe[:, 0:t1 - t0, :], qp[:, 0:t1 - t0, :], emb[:, c % NBUF, t0:t1, :],
                                        ALU.mult).then_inc(qe_done, 1)
                dve.wait_ge(qe_done, g)
                nc.vector.tensor_reduce(var[:, t0:t1], qe[:, 0:t1 - t0, :], AX.X, ALU.add).then_inc(var_ok, 1)

            def scale_rows(c, a):
                t0, t1 = GROUP[a]
                g = 2 * c + a + 1
                dve.wait_ge(std_ok, g)
                nc.vector.reciprocal(rstd[:, t0:t1], std[:, t0:t1]).then_inc(rstd_ok, 1)
                dve.wait_ge(rstd_ok, g)
                nc.vector.tensor_tensor(
                    es[:, c % 2, t0:t1, :], emb[:, c % NBUF, t0:t1, :],
                    rstd[:, t0:t1].unsqueeze(2).broadcast_to([P, t1 - t0, D]), ALU.mult).then_inc(es_ok, 1)

            def low_part(c, a):
                t0, t1 = GROUP[a]
                dve.wait_ge(es_hi_ok, 2 * c + a + 1)
                nc.vector.tensor_tensor(es2[:, c % 2, t0:t1, 1, :], es[:, c % 2, t0:t1, :],
                                        es2[:, c % 2, t0:t1, 0, :].bitcast(F32), ALU.subtract).then_inc(es2_ok, 1)

            for n in range(SLOTS):
                m = n - LV
                if 0 <= m < N:
                    dve.wait_ge(u_copied, m + 1)
                    nc.vector.tensor_tensor(u2[0:D, m % 2, :], up[m % 2][0:D, :], u1[0:D, m % 2, :].bitcast(F32),
                                            ALU.subtract).then_inc(u2_ok, 1)
                m = n - LV - 1
                if 0 <= m < N:
                    dve.wait_ge(sq_ok, m + 1)
                    nc.vector.tensor_reduce(ss[:, m % 2, :], vsq[:, m % 2, :].rearrange("p (s q) -> p s q", s=WIN),
                                            AX.X, ALU.add).then_inc(ss_ok, 1)
                for piece, late in ((low_part, 4), (scale_rows, 3), (row_statistics, 2)):
                    for a in range(2):
                        c, w = divmod(n - late - 2 * a, NW)
                        if w == 0 and 0 <= c < NC:
                            piece(c, a)
                if n == 2:
                    finish_x()
                if n == 3:
                    pair_coefficients()
                k = block_at(n, 0)
                if k is not None:
                    dve.wait_ge(g_copied, 2 * NW * (k + 1))
                    if k >= 1:
                        dve.wait_ge(f5_ok, k)
                    else:
                        dve.wait_ge(fill_ok, 7)
                        dve.wait_ge(a_s, 1)
                    nc.vector.transpose(zt[:, :, 0:PROJ], zs[:, :, :].rearrange("p g c -> p c g")).then_inc(zt_ok, 1)
                    nc.vector.tensor_copy(ZT[:, PROJ:PROJ + 1], sumx[:, k:k + 1]).then_inc(zt_ok, 1)
                k = block_at(n, 5)
                if k is not None:
                    dve.wait_ge(o_sd, k + 1)
                    nc.vector.reciprocal(ost[:, 2:3], ost[:, 1:2]).then_inc(o_r, 1)
                k = block_at(n, 6)
                if k is not None:
                    dve.wait_ge(z_t, k + 1)
                    if k == 0:
                        dve.wait_ge(ld_top, 16 * 6)
                    for i in range(3):
                        nc.vector.tensor_scalar(zn[:, i, :], fp[:, i * BLK:(i + 1) * BLK], gl_c[:, i:i + 1],
                                                bl_c[:, i:i + 1], ALU.mult, ALU.add).then_inc(z_c, 1)
                k = block_at(n, 8)
                if k is not None:
                    dve.wait_ge(m1_done, k + 1)
                    if k == 0:
                        dve.wait_ge(hd_ok, 4)
                    nc.vector.tensor_tensor(h1s[:, :, :], fp.rearrange("p (i b) -> p i b", i=4),
                                            h1d[:, :, k * BLK:(k + 1) * BLK], ALU.add).then_inc(hs_ok, 1)
                k = block_at(n, 10)
                if k is not None:
                    dve.wait_ge(m3_done, k + 1)
                    nc.vector.tensor_copy(y_sb[:, k * BLK:(k + 1) * BLK], fp[0:1, 0:BLK]).then_inc(y_ok, 1)
                m = n - LV - 1
                if 0 <= m < N:
                    dve.wait_ge(sd_ok, m + 1)
                    nc.vector.reciprocal(r2[:, m % 2, :], sd[:, m % 2, :]).then_inc(r2_ok, 1)
                    dve.wait_ge(r2_ok, m + 1)
                    cm, wm = divmod(m, NW)
                    nc.vector.tensor_tensor(
                        T[:, cm % 2, WIN * wm:WIN * (wm + 1), 2:C],
                        vp[m % 2].rearrange("p (s q) -> p s q", s=WIN),
                        r2[:, m % 2, :].unsqueeze(2).broadcast_to([P, WIN, PROJ]), ALU.mult).then_inc(t_ok, 1)

        @block.scalar
        def _(act):
            act.wait_ge(p_wce, 1)
            nc.scalar.activation(wce[:, :], fp[:, 0:P], ACT.Copy).then_inc(a_wce, 1)
            act.wait_ge(p_gram, 1)
            act.wait_ge(fill_ok, 5)
            for h in range(2):
                half = slice(D * h, D * h + D)
                nc.scalar.activation(gram[half, half], fp[half, P:P + D], ACT.Copy, scale=1.0 / E).then_inc(a_gram, 1)
            act.wait_ge(p_sw, 1)
            nc.scalar.activation(sw[SHIFT_ROWS, 0, :], up[0][SHIFT_ROWS, 0:PROJ], ACT.Copy).then_inc(a_sw, 1)
            centred = [0]

            def centre(dst, src, scratch, total):
                at = centred[0]
                nc.scalar.activation(scratch, src, ACT.Copy, accum_out=total[:, 0:1]).then_inc(wlc_ok, 1)
                act.wait_ge(wlc_ok, at + 1)
                nc.scalar.mul(total[:, 1:2], total[:, 0:1], -1.0 / MAXD).then_inc(wlc_ok, 1)
                act.wait_ge(wlc_ok, at + 2)
                nc.scalar.activation(dst, src, ACT.Identity, bias=total[:, 1:2]).then_inc(wlc_ok, 1)
                act.wait_ge(wlc_ok, at + 3)
                centred[0] += 3

            def std_of_rows(c, a):
                t0, t1 = GROUP[a]
                act.wait_ge(var_ok, 2 * c + a + 1)
                nc.scalar.activation(std[:, t0:t1], var[:, t0:t1], ACT.Sqrt, bias=eps[:, 0:1]).then_inc(std_ok, 1)

            def high_part(c, a):
                t0, t1 = GROUP[a]
                act.wait_ge(es_ok, 2 * c + a + 1)
                nc.scalar.activation(es2[:, c % 2, t0:t1, 0, :], es[:, c % 2, t0:t1, :], ACT.Copy).then_inc(es_hi_ok, 1)

            for n in range(SLOTS):
                c, w = divmod(n, NW)
                m = n - LG - 1
                if 0 <= m < N:
                    act.wait_ge(g_done, m + 1)
                    if m % (2 * NW) == 0 and m:
                        act.wait_ge(zt_ok, 2 * (m // (2 * NW)))
                    g0 = NG * (m % (2 * NW))
                    nc.scalar.activation(
                        zs[:, g0:g0 + NG, :],
                        gp[:, 0:GPW].rearrange("p (g c) -> p g c", g=NG),
                        ACT.Copy).then_inc(g_copied, 1)
                for piece, late in ((high_part, 4), (std_of_rows, 3)):
                    for a in range(2):
                        cc, ww = divmod(n - late - 2 * a, NW)
                        if ww == 0 and 0 <= cc < NC:
                            piece(cc, a)
                k = block_at(n, 9)
                if k is not None:
                    act.wait_ge(hs_ok, k + 1)
                    nc.scalar.activation(h1[:, :, :], h1s[:, :, :], ACT.Relu).then_inc(h1_ok, 1)
                k = block_at(n, 10)
                if k is not None:
                    act.wait_ge(m2_done, k + 1)
                    for i in range(2):
                        nc.scalar.activation(h2[:, i, :], fp[:, i * BLK:(i + 1) * BLK], ACT.Relu,
                                             bias=b2_c[:, i:i + 1]).then_inc(h2_ok, 1)
                if c < NC:
                    act.wait_ge(et_t, n + 1)
                    k = block_at(n, 3)
                    if k is not None:
                        act.wait_ge(f5_t, k + 1)
                        nc.scalar.activation(zf[0:FEAT5, NQ, :], etp[0:FEAT5, 2, :], ACT.Copy).then_inc(f5_ok, 1)
                    p0, np_ = PAIRS[w][0], len(PAIRS[w])
                    nc.scalar.activation(et[:, p0:p0 + np_, :], etp[:, 0:np_, :], ACT.Copy).then_inc(et_c, 1)
                k = block_at(n, 3)
                if k is not None:
                    act.wait_ge(f_t, k + 1)
                    nc.scalar.activation(zf[:, 0:NQ, :], fp.rearrange("p (i b) -> p i b", i=NQ), ACT.Copy).then_inc(f_c, 1)
                    if c >= NC:
                        act.wait_ge(f5_t, k + 1)
                        nc.scalar.activation(zf[0:FEAT5, NQ, :], etp[0:FEAT5, 2, :], ACT.Copy).then_inc(f5_ok, 1)
                k = block_at(n, 5)
                if k is not None:
                    act.wait_ge(o_done, k + 1)
                    nc.scalar.activation(osq[:, :], fp, ACT.Square, accum_out=ost[:, 0:1]).then_inc(o_ss, 1)
                    act.wait_ge(o_ss, k + 1)
                    nc.scalar.activation(ost[:, 1:2], ost[:, 0:1], ACT.Sqrt, bias=eps[:, 0:1],
                                         scale=1.0 / MAXD).then_inc(o_sd, 1)
                m = n - LV - 1
                if 0 <= m < N:
                    act.wait_ge(ss_ok, m + 1)
                    nc.scalar.activation(sd[:, m % 2, :], ss[:, m % 2, :], ACT.Sqrt, bias=eps[:, 0:1],
                                         scale=1.0 / PROJ).then_inc(sd_ok, 1)
                m = n - LC
                if 0 <= m < N:
                    act.wait_ge(u_done, m + 1)
                    nc.scalar.activation(u1[:, m % 2, :], up[m % 2], ACT.Copy).then_inc(u_copied, 1)
                if w == 0 and 0 < c <= NC:
                    if c == 1:
                        act.wait_ge(xt_ok, 1)
                    k, h = divmod(c - 1, 2)
                    nc.scalar.activation(
                        T[:, (c - 1) % 2, :, 0].rearrange("p (g j) -> p g j", j=4),
                        xt[:, k * BLK:(k + 1) * BLK].rearrange("p (j g) -> p g j", j=4)[:, 16 * h:16 * h + 16, :],
                        ACT.Copy).then_inc(x_in, 1)
                if n < 4:
                    act.wait_ge(hd_done, n + 1)
                    nc.scalar.activation(h1d[:, n, :], hd_bank[n], ACT.Identity, bias=b1_c[:, n:n + 1]).then_inc(hd_ok, 1)
                if n == 0:
                    act.wait_ge(p_x, 1)
                    nc.scalar.activation(xsq[:, :], vp[0], ACT.Square).then_inc(a_xsq, 1)
                if n == 1:
                    act.wait_ge(p_xv, 1)
                    act.wait_ge(fill_ok, 3)
                    nc.scalar.activation(xsd[:, :], vp[1], ACT.Sqrt, bias=eps[:, 0:1]).then_inc(a_xsd, 1)
                if n == 5:
                    act.wait_ge(p_s, 1)
                    nc.scalar.activation(sumx[:, :], fp[:, 0:NK], ACT.Copy).then_inc(a_s, 1)
                if n in WL_SLOTS[:NQ]:
                    i = WL_SLOTS.index(n)
                    if i == 0:
                        act.wait_ge(ld_wl, 80)
                        act.wait_ge(cf_ok, 1)
                    centre(wlc[:, i, :], wl_sb[:, i, :], wlm[:, i, :], lsum[:, 2 * i:2 * i + 2])
                    nc.scalar.activation(wlm[:, i, :], wlc[:, i, :], ACT.Copy, scale=cf[:, 0, i:i + 1]).then_inc(wl_ok, 1)
                if n == WL_SLOTS[NQ]:
                    centre(wlxc[:, :], wlx_sb[:, :], wl5[0:PROJ, :], lsum[0:PROJ, 8:10])
                if n == W5_SLOT:
                    act.wait_ge(p_w5, 1)
                    nc.scalar.activation(wl5[:, :], fp[0:FEAT5, :], ACT.Copy).then_inc(a_w5, 1)
                k = block_at(n, 1)
                if k is not None:
                    act.wait_ge(zt_ok, 2 * k + 1)
                    nc.scalar.activation(zt[:, 2:C, PROJ:ROW], zt[:, 2:C, 0:WRAP], ACT.Copy).then_inc(zw_ok, 1)
                    act.wait_ge(zw_ok, 2 * k + 1)
                    at = 2 * ROW + 1
                    nc.scalar.activation(
                        zp[:, :, :],
                        ZT[:, at:at + (ROW + 1) * PROJ].rearrange("p (q r) -> p q r", q=PROJ)[:, :, 0:WRAP],
                        ACT.Copy).then_inc(zw_ok, 1)
                k = block_at(n, 5)
                if k is not None:
                    act.wait_ge(o_r, k + 1)
                    nc.scalar.activation(on[:, :], fp[:, 0:USED], ACT.Copy, scale=ost[:, 2:3]).then_inc(on_ok, 1)
                m = n - LV
                if 0 <= m < N:
                    act.wait_ge(v_done, m + 1)
                    if m >= 2:
                        act.wait_ge(ss_ok, m - 1)
                    nc.scalar.activation(vsq[:, m % 2, :], vp[m % 2], ACT.Square).then_inc(sq_ok, 1)

        @block.tensor
        def _(pe):
            pe.wait_ge(ld_const, 16)
            pe.wait_ge(wc_ok, 1)
            nc.tensor.transpose(fp[:, 0:P], wc[:, :], ident).then_inc(p_wce, 1)
            pe.wait_ge(a_wce, 1)
            nc.tensor.matmul(fp[:, P:P + D], wce[:, :], wce[:, 0:D], start=True, stop=True).then_inc(p_gram, 1)
            pe.wait_ge(mix_ok, 1)
            pe.wait_ge(fill_ok, 3)
            nc.tensor.matmul(up[0][:, 0:PROJ], ones_1[0:N_TBL, :], wsic[0:N_TBL, 0, :],
                             start=True, stop=True).then_inc(p_sw, 1)
            pe.wait_ge(a_gram, 2)
            pe.wait_ge(a_sw, 1)

            for n in range(SLOTS):
                c, w = divmod(n, NW)
                k = block_at(n, 3)
                if k is not None:
                    pe.wait_ge(et_c, min(n, N))
                    nc.tensor.transpose(etp[0:FEAT5, 2, :], ZT[:, 0:FEAT5], ident).then_inc(f5_t, 1)
                if c < NC:
                    for p in PAIRS[w]:
                        t0 = min(2 * p, TILES - 2)
                        pe.wait_ge(gath[c % NBUF][p], (c // NBUF + 1) * (32 if 2 * p + 1 < TILES else 16))
                        if n and p == PAIRS[w][0]:
                            pe.wait_ge(et_c, n)
                        last = nc.tensor.transpose(etp[:, p - PAIRS[w][0], :],
                                                   emb[:, c % NBUF, t0:t0 + 2, :].rearrange("p t d -> p (t d)"),
                                                   ident)
                    last.then_inc(et_t, 1)
                k = block_at(n, 6)
                if k is not None:
                    pe.wait_ge(on_ok, k + 1)
                    for i in range(3):
                        last = nc.tensor.transpose(fp[:, i * BLK:(i + 1) * BLK], on[:, i * BLK:(i + 1) * BLK], ident)
                    last.then_inc(z_t, 1)
                k = block_at(n, 10)
                if k is not None:
                    pe.wait_ge(h2_ok, 2 * k + 2)
                    for kk in range(2):
                        last = nc.tensor.matmul(fp[0:1, 0:BLK], w3_c[:, kk:kk + 1], h2[:, kk, :],
                                                start=(kk == 0), stop=(kk == 1))
                    last.then_inc(m3_done, 1)
                if 1 <= n <= N:
                    cq, wq = divmod(n - 1, NW)
                    pe.wait_ge(et_c, n)
                    for p in PAIRS[wq]:
                        a = int(2 * p >= GROUP[1][0])
                        if 2 * p == GROUP[a][0] and 2 * cq + a:
                            pe.wait_ge(qe_done, 2 * cq + a)
                        at, lone = 2 * p - GROUP[a][0], 2 * p + 1 == TILES
                        last = nc.tensor.matmul(
                            qp[:, at:at + 2 - lone, :], et[:, p, :], gram[:, D * lone:], start=True, stop=True)
                        if p == PAIRS[1][-1] or lone:
                            last.then_inc(q_done, 1)
                m = n - LC
                if 0 <= m < N:
                    cm, wm = divmod(m, NW)
                    pe.wait_ge(es2_ok, 2 * cm + (2 if wm >= 2 else 1))
                    if m == 0:
                        pe.wait_ge(mix_ok, 3)
                    if m >= 2:
                        pe.wait_ge(u2_ok, m - 1)
                    tiles = pieces(wm)
                    for i, (t, s0, ns, at) in enumerate(tiles):
                        rows = es2[:, cm % 2, t, :, :].rearrange("p h d -> p (h d)")
                        for part in (mix_hi, mix_lo):
                            last = nc.tensor.matmul(
                                up[m % 2][:, PROJ * s0:PROJ * (s0 + ns)], rows,
                                part[:, t, at:at + ns, :].rearrange("p b q -> p (b q)"),
                                start=(i == 0 and part is mix_hi),
                                stop=(i == len(tiles) - 1 and part is mix_lo), skip_group_check=True)
                    last.then_inc(u_done, 1)
                m = n - LV
                if 0 <= m < N:
                    pe.wait_ge(u2_ok, m + 1)
                    if m == 0:
                        pe.wait_ge(wc_ok, 4)
                        pe.wait_ge(xt_ok, 1)
                    if m >= 2:
                        pe.wait_ge(t_ok, m - 1)
                    nc.tensor.matmul(vp[m % 2], wg_hi[:, :], u1[:, m % 2, :], start=True, stop=False)
                    nc.tensor.matmul(vp[m % 2], wg_lo[:, :], u1[:, m % 2, :], start=False, stop=False)
                    nc.tensor.matmul(vp[m % 2], wg_bs[:, :], u2[:, m % 2, :], start=False, stop=True).then_inc(v_done, 1)
                m = n - LG
                if 0 <= m < N:
                    cm, wm = divmod(m, NW)
                    pe.wait_ge(t_ok, m + 1)
                    pe.wait_ge(x_in, cm + 1)
                    if m == 0:
                        pe.wait_ge(fill_ok, 4)
                    if m >= 1:
                        pe.wait_ge(g_copied, m)
                    for g in range(NG):
                        for j in range(4):
                            s = WIN * wm + 4 * g + j
                            at = C * g
                            last = nc.tensor.matmul(gp[32 * j:32 * j + 32, at:at + C], T[:, cm % 2, s, 2:C],
                                                    T[:, cm % 2, s, :], start=True, stop=True)
                    last.then_inc(g_done, 1)
                if n < 4:
                    if n == 0:
                        pe.wait_ge(ld_x, 32)
                        pe.wait_ge(ld_dense, 32)
                    for i in range(2):
                        last = nc.tensor.matmul(hd_bank[n], w1_sb[:, 3 + i, n * P:(n + 1) * P], dn[:, i, :],
                                                start=(i == 0), stop=(i == 1))
                    last.then_inc(hd_done, 1)
                if n == 0:
                    pe.wait_ge(wd_ok, 1)
                    for i in range(2):
                        last = nc.tensor.matmul(vp[0], wdc[:, i, :], dn[:, i, :], start=(i == 0), stop=(i == 1))
                    last.then_inc(p_x, 1)
                if n == 1:
                    pe.wait_ge(a_xsq, 1)
                    nc.tensor.matmul(vp[1], ones_e[:, :], xsq[:, :], start=True, stop=True).then_inc(p_xv, 1)
                if n == 4:
                    pe.wait_ge(xt_ok, 1)
                    pe.wait_ge(hd_ok, 4)
                    for k in range(NK):
                        last = nc.tensor.matmul(fp[:, k:k + 1], xt[:, k * BLK:(k + 1) * BLK], ones_1[:, 0:1],
                                                start=True, stop=True)
                    last.then_inc(p_s, 1)
                if n == W5_SLOT:
                    pe.wait_ge(a_s, 1)
                    pe.wait_ge(m_ok, 1)
                    pe.wait_ge(wlc_ok, 3 * (NQ + 1))
                    for i in range(NQ):
                        nc.tensor.matmul(fp[0:FEAT5, :], mm[:, i, :], wlc[:, i, :], start=(i == 0), stop=False)
                    nc.tensor.matmul(fp[0:FEAT5, :], mmx[:, :], wlxc[:, :], start=False, stop=True).then_inc(p_w5, 1)
                k = block_at(n, 3)
                if k is not None:
                    pe.wait_ge(f_c, k + 1)
                    for i in range(2):
                        nc.tensor.matmul(fp, zf[:, i, :], wlm[:, i, :], start=(i == 0), stop=False)
                k = block_at(n, 4)
                if k is not None:
                    pe.wait_ge(f5_ok, k + 1)
                    for i in range(2, NQ):
                        nc.tensor.matmul(fp, zf[:, i, :], wlm[:, i, :], start=False, stop=False)
                    nc.tensor.matmul(fp, zf[0:FEAT5, NQ, :], wl5[:, :], start=False, stop=True).then_inc(o_done, 1)
                k = block_at(n, 7)
                if k is not None:
                    pe.wait_ge(z_c, 3 * k + 3)
                    for i in range(4):
                        for kk in range(3):
                            last = nc.tensor.matmul(fp[:, i * BLK:(i + 1) * BLK], w1_sb[:, kk, i * P:(i + 1) * P],
                                                    zn[:, kk, :], start=(kk == 0), stop=(kk == 2))
                    last.then_inc(m1_done, 1)
                k = block_at(n, 9)
                if k is not None:
                    pe.wait_ge(h1_ok, k + 1)
                    for i in range(2):
                        for kk in range(4):
                            last = nc.tensor.matmul(fp[:, i * BLK:(i + 1) * BLK], w2_sb[:, kk, i * P:(i + 1) * P],
                                                    h1[:, kk, :], start=(kk == 0), stop=(kk == 3))
                    last.then_inc(m2_done, 1)
                k = block_at(n, 2)
                if k is not None:
                    pe.wait_ge(zw_ok, 2 * k + 2)
                    if k == 0:
                        pe.wait_ge(a_w5, 1)
                        pe.wait_ge(wl_ok, NQ)
                    if k >= 1:
                        pe.wait_ge(y_ok, k)
                    for i in range(NQ):
                        src = zp[:, QT * i:QT * (i + 1), :].rearrange("p q r -> p (q r)")
                        last = nc.tensor.transpose(fp[:, i * BLK:(i + 1) * BLK], src, ident)
                    last.then_inc(f_t, 1)


def layouts(inputs):
    f = {k: np.asarray(v) for k, v in inputs.items()}
    a = {}
    a["tables"] = np.concatenate([f[f"tbl_{i}"] for i in range(N_TBL)], 0)
    s = np.arange(B)
    order = s // BLK * BLK + 32 * (s % 4) + s % BLK // 4
    a["ids"] = f["ids"][order].reshape(NC * TILES, P).T
    starts = np.concatenate([[0], np.cumsum(VOCAB)[:-1]]).astype(a["ids"].dtype)
    a["base"] = np.tile(starts, B).reshape(NC * TILES, P).T
    rows = np.arange(TILES * P).reshape(TILES, P)
    mask = (rows // N_TBL - (rows[:, :1] // N_TBL))[:, :, None] == np.arange(TOUCH)
    q, k = np.meshgrid(np.arange(PROJ), 1 + np.arange(WRAP), indexing="ij")
    p = (q + k) % PROJ
    used = ~((k == WRAP) & (q >= WRAP))
    q, p, used = (x.reshape(NQ, P) for x in (q, p, used))
    hot = lambda x: (ROW + x[:, :, None] == np.arange(FEAT5)).transpose(1, 0, 2).reshape(P, -1)
    pick = np.zeros((P, 4))
    pick[SHIFT_ROWS] = [[1, 0, 1, 0], [1, 0, 0, 1], [0, 1, 1, 0]]
    a["consts"] = np.concatenate(
        [np.eye(P), mask.transpose(1, 0, 2).reshape(P, -1), hot(q), hot(p), pick], 1).astype(np.float32)
    a["wst"] = np.concatenate([f["L0_rec_Ws"].T] * 2, 0)
    a["wsi_rows"] = f["L0_rec_Wsi"].T[rows % N_TBL].transpose(1, 0, 2)
    a["gs"], a["bs"] = f["L0_rec_gs"][None], f["L0_rec_bs"][None]
    gsi, bsi = f["L0_rec_gsi"], f["L0_rec_bsi"]
    a["gsi_pairs"] = np.stack([gsi[q], gsi[p], bsi[q], bsi[p]]).transpose(2, 0, 1)
    a["gsi"], a["bsi"] = gsi[:, None], bsi[:, None]
    wl = f["L0_rec_Wl"].T
    i, j = np.maximum(p, q) + 1, np.minimum(p, q) + 1
    a["wlt"] = np.where(used[:, :, None], wl[i * (i - 1) // 2 + j], np.float32(0)).transpose(1, 0, 2)
    i = np.arange(PROJ) + 1
    a["wlx"] = wl[i * (i - 1) // 2]
    tiles = lambda x: x.reshape(-1, P, x.shape[-1]).transpose(1, 0, 2)
    cols = lambda x: x.reshape(-1, P).T
    a["dense_t"] = tiles(f["r_dense_t"].T)
    a["wdt"] = tiles(f["L0_rec_Wd"].T)
    a["gd"], a["bd"] = cols(f["L0_rec_gd"]), cols(f["L0_rec_bd"])
    a["gl"], a["bl"] = cols(f["L0_rec_gl"][:USED]), cols(f["L0_rec_bl"][:USED])
    w1 = f["W_top1"]
    a["w1"] = tiles(np.concatenate([w1[:USED], w1[MAXD:]], 0))
    a["b1"] = cols(f["b_top1"])
    a["w2"] = tiles(f["W_top2"])
    a["b2"] = cols(f["b_top2"])
    a["w3"] = cols(f["W_top3"][:, 0])
    return {"in_" + n: np.ascontiguousarray(x) for n, x in a.items()}


def kernel(**inputs):
    import concourse.bacc as bacc
    from concourse.bass_utils import run_bass_kernel_spmd

    arrays = layouts(inputs)
    nc = bacc.Bacc("TRN2", target_bir_lowering=False, num_devices=1)
    args = []
    for name, x in arrays.items():
        ap = nc.dram_tensor(name, x.shape, mybir.dt.from_np(x.dtype), kind="ExternalInput").ap()
        args.append(ap.bitcast(U32) if x.dtype.kind == "i" else ap)
    out = nc.dram_tensor("out_0", (1, B), F32, kind="ExternalOutput").ap()
    tower(nc, *args, out)
    got = run_bass_kernel_spmd(nc, [arrays], core_ids=[0])
    return got.results[0]["out_0"].reshape(B, 1)
```

```python
from contextlib import ExitStack

import concourse.bass as bass
import numpy as np
from concourse import mybir

F32 = mybir.dt.float32
F32R = mybir.dt.float32r
U32 = mybir.dt.uint32
ALU = mybir.AluOpType
ACT = mybir.ActivationFunctionType
AX = mybir.AxisListType

P = 128
B, N_TBL, D, E, PROJ = 512, 26, 64, 128, 32
VOCAB = [125000, 125000, 12500, 12500, 125000, 12500, 12500, 1000, 12500, 1250, 12500, 1000, 12500,
         1000, 1250, 1250, 1250, 12500, 1250, 1000, 1250, 1000, 1000, 1250, 1000, 1250]
MAXD, USED, D_DENSE = 512, 384, 256
H1, H2 = 512, 256
EPS = 1e-5

CHUNK = 64
NC = B // CHUNK
TILES = CHUNK * N_TBL // P
WIN = 16
NW = CHUNK // WIN
HALF = WIN // 2
HP = HALF * PROJ
NG = WIN // 4
BLK = 128
NK = B // BLK
TOUCH = 6
C = PROJ + 2
WRAP = PROJ // 2
ROW = PROJ + WRAP
FEAT5 = ROW + PROJ
ONE = PROJ + 1
HALVES = [slice(0, D), slice(D, P)]
NQ = 4
QT = PROJ // NQ
PAIRS = [[0, 1], [2, 3], [4], [5, 6]]
NPAIR = 7
NBUF = 3
GROUP = [(0, 8), (8, TILES)]


SHIFT_ROWS = slice(0, 3)


def first_sample(t):
    return P * t // N_TBL


def pieces(h):
    out = []
    for t in range(TILES):
        lo, hi = first_sample(t), (P * t + P - 1) // N_TBL + 1
        a, b = max(lo, HALF * h), min(hi, HALF * (h + 1))
        if a < b:
            out.append((t, a - HALF * h, b - a, a - lo))
    return out


def tower(nc, tables, ids, base, consts, wst, wsi_rows, gs, bs, gsi_pairs, gsi, bsi, wlt, wlx,
          dense_t, wdt, gd, bd, gl, bl, w1, b1, w2, b2, w3, out):
    ctx = ExitStack()
    with ctx:
        def sb(name, shape, dt=F32):
            return ctx.enter_context(nc.sbuf_tensor(name, shape, dt))

        def sem(name):
            return ctx.enter_context(nc.semaphore(name))

        ids_sb = sb("ids_sb", [P, NC * TILES], U32)
        base_sb = sb("base_sb", [P, NC * TILES], U32)
        idx = sb("idx", [P, NC * TILES], U32)
        NCONST = P + TILES * TOUCH + 2 * NQ * FEAT5 + 4
        const_sb = sb("const_sb", [P, NCONST])
        ident = const_sb[:, 0:P]
        mask = const_sb[:, P:P + TILES * TOUCH].rearrange("p (t b) -> p t b", t=TILES)
        hot_at = P + TILES * TOUCH
        hot_q = const_sb[:, hot_at:hot_at + NQ * FEAT5].rearrange("p (i c) -> p i c", i=NQ)
        hot_p = const_sb[:, hot_at + NQ * FEAT5:NCONST - 4].rearrange("p (i c) -> p i c", i=NQ)
        pick = const_sb[SHIFT_ROWS, NCONST - 4:NCONST]
        wst_sb = sb("wst_sb", [P, E])
        wc = sb("wc", [P, E])
        wce = sb("wce", [E, P])
        gram = sb("gram", [P, 2 * D])
        gs_sb = sb("gs_sb", [P, E])
        wg = sb("wg", [P, E])
        wg_hi = sb("wg_hi", [P, E], F32R)
        wg_lo = sb("wg_lo", [P, E], F32R)
        bs3 = sb("bs3", [P, E], F32R)
        sw3 = sb("sw3", [P, WIN, PROJ], F32R)
        bs_sb = sb("bs_sb", [3, 4, E])
        bs_hi = sb("bs_hi", [3, E], F32R)
        sw = sb("sw", [3, 4, PROJ])
        sw_hi = sb("sw_hi", [3, PROJ], F32R)
        wsi_sb = sb("wsi_sb", [P, TILES, PROJ])
        wsic = sb("wsic", [P, TILES, PROJ])
        mix = sb("mix", [P, TILES, TOUCH, PROJ])
        pp_sb = sb("pp_sb", [P, 4, NQ])
        cf = sb("cf", [P, 4, NQ])
        gsi_sb = sb("gsi_sb", [PROJ, 1])
        bsi_sb = sb("bsi_sb", [PROJ, 1])
        wl_sb = sb("wl_sb", [P, NQ, MAXD])
        wlc = sb("wlc", [P, NQ, MAXD])
        wlm = sb("wlm", [P, NQ, MAXD])
        wlx_sb = sb("wlx_sb", [PROJ, MAXD])
        wlxc = sb("wlxc", [PROJ, MAXD])
        mm = sb("mm", [P, NQ, FEAT5])
        mmx = sb("mmx", [PROJ, FEAT5])
        mt = sb("mt", [P, NQ, FEAT5])
        wl5 = sb("wl5", [FEAT5, MAXD])
        dn = sb("dn", [P, 2, B])
        wd_sb = sb("wd_sb", [P, 2, E])
        wdc = sb("wdc", [P, 2, E])
        vec = sb("vec", [P, 2 + 3 + 3 + 4 + 2 + 2])
        gd_c, bd_c = vec[:, 0:1], vec[:, 1:2]
        gl_c, bl_c = vec[:, 2:5], vec[:, 5:8]
        b1_c, b2_c, w3_c = vec[:, 8:12], vec[:, 12:14], vec[:, 14:16]
        w1_sb = sb("w1_sb", [P, 5, H1])
        w2_sb = sb("w2_sb", [P, 4, H2])
        sums = sb("sums", [P, 64])
        ones_e = sb("ones_e", [P, P])
        ones_1 = sb("ones_1", [P, P])
        eps = sb("eps", [P, 1])
        lsum = sb("lsum", [P, 10])
        xsq = sb("xsq", [P, B])
        xsd = sb("xsd", [P, B])
        xr = sb("xr", [P, B])
        xn = sb("xn", [P, B])
        xt = sb("xt", [P, B])
        sumx = sb("sumx", [P, NK])

        emb = sb("emb", [P, NBUF, TILES, D])
        et = sb("et", [P, NPAIR, P])
        qe = sb("qe", [P, 8, D])
        var = sb("var", [P, TILES])
        std = sb("std", [P, TILES])
        rstd = sb("rstd", [P, TILES])
        es = sb("es", [P, 2, TILES, D])
        u = sb("u", [P, 2, 2, HP], F32R)
        vsq = sb("vsq", [P, 2, WIN * PROJ])
        ss = sb("ss", [P, 2, WIN])
        sd = sb("sd", [P, 2, WIN])
        r2 = sb("r2", [P, 2, WIN])
        T = sb("T", [P, 2, CHUNK, C])
        zs = sb("zs", [P, 2, BLK // 4, C])
        ZT = sb("ZT", [P, ROW * (C + 1)])
        zt = ZT[:, 0:ROW * C].rearrange("p (c q) -> p c q", c=C)
        zp = sb("zp", [P, PROJ, WRAP])
        zf = sb("zf", [P, NQ + 1, BLK])
        osq = sb("osq", [P, MAXD])
        ost = sb("ost", [P, 3])
        on = sb("on", [P, USED])
        zn = sb("zn", [P, 3, BLK])
        h1d = sb("h1d", [P, 4, B])
        h1s = sb("h1s", [P, 4, BLK])
        h1 = sb("h1", [P, 4, BLK])
        h2 = sb("h2", [P, 2, BLK])
        y_sb = sb("y_sb", [1, B])

        ps = ctx.enter_context(nc.psum_tensor("ps", [P, 8, 512], F32))
        etp = ps[:, 0, :].rearrange("p (u r) -> p u r", u=4)
        qp = ps[:, 1, :].rearrange("p (t d) -> p t d", d=D)
        up = [ps[:, 2, :], ps[:, 3, :]]
        vp = [ps[:, 4, :], ps[:, 5, :]]
        gp = ps[:, 6, :]
        fp = ps[:, 7, :]
        hd_bank = [up[0], up[1], gp, fp]
        qp_bank = ps[:, 1, :]
        shift_rows = sw3[:, :, :].rearrange("p s q -> p (s q)")
        GPW = NG * C

        ld_ids, ld_const, ld_ws, ld_wsi, ld_x, ld_dense, ld_vec, ld_wl, ld_top = [
            sem(n) for n in ("ld_ids", "ld_const", "ld_ws", "ld_wsi", "ld_x", "ld_dense", "ld_vec", "ld_wl", "ld_top")]
        gath = [[sem(f"gath{a}_{i}") for i in range(NPAIR)] for a in range(NBUF)]
        prep = sem("prep")
        idx_ok, zero_ok, wc_ok, mix_ok, wd_ok, fill_ok, m_ok = [
            sem(n) for n in ("idx_ok", "zero_ok", "wc_ok", "mix_ok", "wd_ok", "fill_ok", "m_ok")]
        p_wce, p_gram, p_sw, p_x, p_xv, p_s, p_w5 = [
            sem(n) for n in ("p_wce", "p_gram", "p_sw", "p_x", "p_xv", "p_s", "p_w5")]
        a_wce, a_gram, a_sw, a_xsq, a_xsd, a_s, a_w5 = [
            sem(n) for n in ("a_wce", "a_gram", "a_sw", "a_xsq", "a_xsd", "a_s", "a_w5")]
        xt_ok, cf_ok, wlc_ok, wl_ok, u2_ok = [
            sem(n) for n in ("xt_ok", "cf_ok", "wlc_ok", "wl_ok", "u2_ok")]
        et_t, et_c, q_done, qe_done, var_ok, std_ok, rstd_ok, es_ok = [
            sem(n) for n in ("et_t", "et_c", "q_done", "qe_done", "var_ok", "std_ok", "rstd_ok", "es_ok")]
        u_done, u_copied, v_done, sq_ok, ss_ok, sd_ok, r2_ok, t_ok = [
            sem(n) for n in ("u_done", "u_copied", "v_done", "sq_ok", "ss_ok", "sd_ok", "r2_ok", "t_ok")]
        x_in, g_done, g_copied, zt_ok, zw_ok, f_t, f_c, f5_t, f5_ok = [
            sem(n) for n in ("x_in", "g_done", "g_copied", "zt_ok", "zw_ok", "f_t", "f_c", "f5_t", "f5_ok")]
        o_done, o_ss, o_sd, o_r, on_ok, z_t, z_c = [
            sem(n) for n in ("o_done", "o_ss", "o_sd", "o_r", "on_ok", "z_t", "z_c")]
        hd_done, hd_ok, m1_done, hs_ok, h1_ok, m2_done, h2_ok, m3_done, y_ok, out_ok = [
            sem(n) for n in ("hd_done", "hd_ok", "m1_done", "hs_ok", "h1_ok", "m2_done", "h2_ok", "m3_done", "y_ok", "out_ok")]

        LC = 4
        LV, LG = LC + 1, LC + 3
        SLOTS = NC * NW + LG + 11
        WL_SLOTS = [4, 5, 7, 9, 10]
        WLM_SLOTS = [6, 8, 11, 12]
        W5_SLOT = 12
        LIGHT = 2 * NW + LG + 3
        N = NC * NW

        def block_at(n, d):
            k, r = divmod(n - d - (2 * NW + LG), 2 * NW)
            if r == 0 and 0 <= k < NK - 1:
                return k
            return NK - 1 if n - d + 1 == 2 * NW * NK + LG else None

        def f_bank(k):
            return fp if k < NK - 1 else up[0]

        block = ctx.enter_context(nc.Block())

        @block.sync
        def _(sp):
            sp.dma_start(ids_sb[:, :], ids).then_inc(ld_ids, 16)
            sp.dma_start(base_sb[:, :], base).then_inc(ld_ids, 16)
            sp.dma_start(wst_sb[:, :], wst).then_inc(ld_ws, 16)
            sp.dma_start(const_sb[:, :], consts).then_inc(ld_const, 16)
            sp.dma_start(gs_sb[:, :], gs.broadcast_to([P, E])).then_inc(ld_ws, 16)
            sp.dma_start(bs_sb[SHIFT_ROWS, 0, :], bs.broadcast_to([3, E])).then_inc(ld_ws, 16)
            sp.dma_start(wsi_sb[:, :, :], wsi_rows).then_inc(ld_wsi, 16)
            sp.dma_start(wd_sb[:, :, :], wdt).then_inc(ld_x, 16)
            sp.dma_start(dn[:, :, :], dense_t).then_inc(ld_x, 16)
            sp.dma_start(w1_sb[:, 3:5, :], w1[:, 3:5, :]).then_inc(ld_dense, 16)
            sp.dma_start(b1_c, b1).then_inc(ld_dense, 16)
            sp.dma_start(gd_c, gd).then_inc(ld_vec, 16)
            sp.dma_start(bd_c, bd).then_inc(ld_vec, 16)
            sp.wait_ge(et_t, 2)
            sp.dma_start(wl_sb[:, :, :], wlt).then_inc(ld_wl, 16)
            sp.dma_start(wlx_sb[:, :], wlx).then_inc(ld_wl, 16)
            sp.dma_start(pp_sb[:, :, :], gsi_pairs).then_inc(ld_wl, 16)
            sp.dma_start(gsi_sb[:, :], gsi).then_inc(ld_wl, 16)
            sp.dma_start(bsi_sb[:, :], bsi).then_inc(ld_wl, 16)
            sp.wait_ge(et_t, 8)
            sp.dma_start(gl_c, gl).then_inc(ld_top, 16)
            sp.dma_start(bl_c, bl).then_inc(ld_top, 16)
            sp.dma_start(b2_c, b2).then_inc(ld_top, 16)
            sp.dma_start(w3_c, w3).then_inc(ld_top, 16)
            sp.dma_start(w1_sb[:, 0:3, :], w1[:, 0:3, :]).then_inc(ld_top, 16)
            sp.dma_start(w2_sb[:, :, :], w2).then_inc(ld_top, 16)
            sp.wait_ge(y_ok, NK)
            sp.dma_start(out, y_sb[:, :]).then_inc(out_ok, 16)
            sp.wait_ge(out_ok, 16)

        @block.gpsimd
        def _(pool):
            pool.wait_ge(idx_ok, 1)
            for c in range(NC):
                if c >= NBUF:
                    pool.wait_ge(es_ok, 2 * (c - NBUF + 1))
                for t in range(TILES):
                    at = c * TILES + t
                    nc.gpsimd.indirect_dma_start(
                        emb[:, c % NBUF, t, :], None, tables,
                        bass.IndirectOffsetOnAxis(ap=idx[:, at:at + 1], axis=0),
                    ).then_inc(gath[c % NBUF][t // 2], 16)

        @block.vector
        def _(dve):
            step = [0]

            def link(ins):
                step[0] += 1
                ins.then_inc(prep, 1)
                dve.wait_ge(prep, step[0])

            def centre(dst, src, total, shape, n):
                link(nc.vector.tensor_reduce(total, src, AX.X, ALU.add))
                link(nc.vector.scalar_tensor_tensor(
                    out=dst, in0=total.unsqueeze(len(shape) - 1).broadcast_to(shape), scalar=-1.0 / n,
                    in1=src, op0=ALU.mult, op1=ALU.add))

            dve.wait_ge(ld_ids, 32)
            nc.vector.tensor_tensor(idx[:, :], ids_sb[:, :], base_sb[:, :], ALU.add).then_inc(idx_ok, 1)
            nc.vector.memset(ones_e[:, :], 1.0 / E).then_inc(fill_ok, 1)
            nc.vector.memset(ones_1[:, :], 1.0).then_inc(fill_ok, 1)
            nc.vector.memset(eps[:, :], EPS).then_inc(fill_ok, 1)
            nc.vector.memset(T[:, :, :, 1:2], 1.0).then_inc(fill_ok, 1)
            nc.vector.memset(gram[:, :], 0.0).then_inc(fill_ok, 1)
            nc.vector.memset(ZT[:, 0:2 * ROW], 0.0).then_inc(fill_ok, 1)
            dve.wait_ge(fill_ok, 2)
            nc.vector.tensor_scalar(bs3[:, :], ones_1[:, 0:E], 0.0, None, ALU.mult).then_inc(zero_ok, 1)
            dve.wait_ge(fill_ok, 6)
            nc.vector.memset(ZT[:, ONE:ONE + 1], 1.0).then_inc(fill_ok, 1)
            nc.vector.tensor_scalar(sw3[:, :, :], ones_1[:, 0:PROJ].unsqueeze(1).broadcast_to([P, WIN, PROJ]), 0.0,
                                    None, ALU.mult).then_inc(zero_ok, 1)
            dve.wait_ge(ld_ws, 48)
            link(nc.vector.tensor_reduce(sums[:, 0:1], wst_sb[:, :], AX.X, ALU.add))
            link(nc.vector.tensor_scalar(sums[:, 1:2], sums[:, 0:1], 1.0 / E, None, ALU.mult))
            nc.vector.tensor_scalar(wc[:, :], wst_sb[:, :], sums[:, 1:2], None, ALU.subtract).then_inc(wc_ok, 1)
            dve.wait_ge(ld_wsi, 16)
            dve.wait_ge(ld_const, 16)
            centre(wsic[:, :, :], wsi_sb[:, :, :], sums[:, 2:2 + TILES], [P, TILES, PROJ], PROJ)
            nc.vector.nop().then_inc(mix_ok, 1)
            dve.wait_ge(ld_x, 32)
            centre(wdc[:, :, :], wd_sb[:, :, :], sums[:, 16:18], [P, 2, E], E)
            nc.vector.nop().then_inc(wd_ok, 1)
            nc.vector.tensor_tensor(
                mix[:, :, :, :], wsic[:, :, :].unsqueeze(2).broadcast_to([P, TILES, TOUCH, PROJ]),
                mask.unsqueeze(3).broadcast_to([P, TILES, TOUCH, PROJ]), ALU.mult).then_inc(mix_ok, 1)
            dve.wait_ge(wc_ok, 1)
            link(nc.vector.tensor_tensor(wg[:, :], wc[:, :], gs_sb[:, :], ALU.mult))
            link(nc.vector.tensor_copy(wg_hi[:, :], wg[:, :]))
            nc.vector.tensor_tensor(wg_lo[:, :], wg[:, :], wg_hi[:, :].bitcast(F32), ALU.subtract).then_inc(wc_ok, 1)

            def three_rows(dst, parts, hi, a):
                link(nc.vector.tensor_copy(hi[SHIFT_ROWS, :], parts[SHIFT_ROWS, 0, :]))
                link(nc.vector.tensor_tensor(parts[SHIFT_ROWS, 1, :], parts[SHIFT_ROWS, 0, :],
                                             hi[SHIFT_ROWS, :].bitcast(F32), ALU.subtract))
                link(nc.vector.tensor_scalar(parts[SHIFT_ROWS, 2, :], parts[SHIFT_ROWS, 1, :], pick[:, a + 1:a + 2],
                                             None, ALU.mult))
                link(nc.vector.scalar_tensor_tensor(
                    out=dst, in0=hi[SHIFT_ROWS, :].bitcast(F32), scalar=pick[:, a:a + 1],
                    in1=parts[SHIFT_ROWS, 2, :], op0=ALU.mult, op1=ALU.add))

            dve.wait_ge(zero_ok, 2)
            three_rows(bs3[SHIFT_ROWS, :], bs_sb, bs_hi, 0)
            dve.wait_ge(a_sw, 1)
            three_rows(sw[SHIFT_ROWS, 3, :], sw, sw_hi, 2)
            nc.vector.tensor_copy(
                sw3[SHIFT_ROWS, :, :], sw[SHIFT_ROWS, 3, :].unsqueeze(1).broadcast_to([3, WIN, PROJ])).then_inc(wc_ok, 1)
            def finish_x():
                dve.wait_ge(ld_vec, 32)
                dve.wait_ge(a_xsd, 1)
                link(nc.vector.reciprocal(xr[:, :], xsd[:, :]))
                link(nc.vector.tensor_tensor(xn[:, :], vp[0], xr[:, :], ALU.mult))
                nc.vector.tensor_scalar(xt[:, :], xn[:, :], gd_c, bd_c, ALU.mult, ALU.add).then_inc(xt_ok, 1)

            def pair_coefficients():
                dve.wait_ge(ld_wl, 80)
                gq, gpr, bq, bp = (pp_sb[:, i, :] for i in range(4))
                nc.vector.tensor_tensor(cf[:, 0, :], gq, gpr, ALU.mult).then_inc(cf_ok, 1)
                link(nc.vector.tensor_tensor(cf[:, 1, :], gq, bp, ALU.mult))
                link(nc.vector.tensor_tensor(cf[:, 2, :], gpr, bq, ALU.mult))
                link(nc.vector.scalar_tensor_tensor(out=cf[:, 3, :], in0=bq, scalar=float(E), in1=bp,
                                                    op0=ALU.mult, op1=ALU.mult))
                link(nc.vector.tensor_tensor(
                    mt[:, :, :], hot_q, cf[:, 1, :].unsqueeze(2).broadcast_to([P, NQ, FEAT5]), ALU.mult))
                link(nc.vector.tensor_tensor(
                    mm[:, :, :], hot_p, cf[:, 2, :].unsqueeze(2).broadcast_to([P, NQ, FEAT5]), ALU.mult))
                link(nc.vector.tensor_tensor(mm[:, :, :], mm[:, :, :], mt[:, :, :], ALU.add))
                link(nc.vector.tensor_copy(mm[:, :, ONE], cf[:, 3, :]))
                link(nc.vector.tensor_scalar(mmx[:, :], const_sb[0:PROJ, 0:FEAT5], gsi_sb[:, :], None, ALU.mult))
                nc.vector.tensor_copy(mmx[:, PROJ:PROJ + 1], bsi_sb[:, :]).then_inc(m_ok, 1)

            def rows_by_gram(c, a):
                t0, t1 = GROUP[a]
                g = 2 * c + a + 1
                dve.wait_ge(q_done, g)
                nc.vector.tensor_tensor(qe[:, 0:t1 - t0, :], qp[:, 0:t1 - t0, :], emb[:, c % NBUF, t0:t1, :],
                                        ALU.mult).then_inc(qe_done, 1)

            def variance(c, a):
                t0, t1 = GROUP[a]
                dve.wait_ge(qe_done, 2 * c + a + 1)
                nc.vector.tensor_reduce(var[:, t0:t1], qe[:, 0:t1 - t0, :], AX.X, ALU.add).then_inc(var_ok, 1)

            def scale_rows(c, a):
                t0, t1 = GROUP[a]
                g = 2 * c + a + 1
                dve.wait_ge(std_ok, g)
                nc.vector.reciprocal(rstd[:, t0:t1], std[:, t0:t1]).then_inc(rstd_ok, 1)
                dve.wait_ge(rstd_ok, g)
                nc.vector.tensor_tensor(
                    es[:, c % 2, t0:t1, :], emb[:, c % NBUF, t0:t1, :],
                    rstd[:, t0:t1].unsqueeze(2).broadcast_to([P, t1 - t0, D]), ALU.mult).then_inc(es_ok, 1)

            for n in range(SLOTS):
                m = n - LV
                if 0 <= m < N:
                    dve.wait_ge(u_copied, 2 * (m + 1))
                    for h, (at, to) in enumerate((HALVES, HALVES[::-1])):
                        nc.vector.tensor_tensor(u[to, m % 2, h, :], up[m % 2][at, 0:HP],
                                                u[at, m % 2, h, :].bitcast(F32), ALU.subtract).then_inc(u2_ok, 1)
                m = n - LV - 1
                if 0 <= m < N:
                    dve.wait_ge(sq_ok, m + 1)
                    nc.vector.tensor_reduce(ss[:, m % 2, :], vsq[:, m % 2, :].rearrange("p (s q) -> p s q", s=WIN),
                                            AX.X, ALU.add).then_inc(ss_ok, 1)
                k = block_at(n, 9)
                if k is not None:
                    dve.wait_ge(m1_done, k + 1)
                    if k == 0:
                        dve.wait_ge(hd_ok, 4)
                    nc.vector.tensor_tensor(h1s[:, :, :], f_bank(k).rearrange("p (i b) -> p i b", i=4),
                                            h1d[:, :, k * BLK:(k + 1) * BLK], ALU.add).then_inc(hs_ok, 1)
                for piece, late in ((variance, 3), (rows_by_gram, 2)):
                    for a in range(2):
                        c, w = divmod(n - late - 2 * a, NW)
                        if w == 0 and 0 <= c < NC:
                            piece(c, a)
                if n == 1:
                    finish_x()
                if n == 5:
                    pair_coefficients()
                k = block_at(n, 1)
                if k is not None:
                    dve.wait_ge(g_copied, 2 * NW * (k + 1))
                    if k >= 1:
                        dve.wait_ge(f5_ok, k)
                    else:
                        dve.wait_ge(fill_ok, 7)
                        dve.wait_ge(a_s, 1)
                    nc.vector.transpose(zt[:, :, 0:PROJ], zs[:, k % 2, :, :].rearrange("p g c -> p c g")).then_inc(zt_ok, 1)
                    nc.vector.tensor_copy(ZT[:, PROJ:PROJ + 1], sumx[:, k:k + 1]).then_inc(zt_ok, 1)
                k = block_at(n, 6)
                if k is not None:
                    dve.wait_ge(o_sd, k + 1)
                    nc.vector.reciprocal(ost[:, 2:3], ost[:, 1:2]).then_inc(o_r, 1)
                m = n - LV - 1
                if 0 <= m < N:
                    dve.wait_ge(sd_ok, m + 1)
                    nc.vector.reciprocal(r2[:, m % 2, :], sd[:, m % 2, :]).then_inc(r2_ok, 1)
                    dve.wait_ge(r2_ok, m + 1)
                    cm, wm = divmod(m, NW)
                    nc.vector.tensor_tensor(
                        T[:, cm % 2, WIN * wm:WIN * (wm + 1), 2:C],
                        vp[m % 2].rearrange("p (s q) -> p s q", s=WIN),
                        r2[:, m % 2, :].unsqueeze(2).broadcast_to([P, WIN, PROJ]), ALU.mult).then_inc(t_ok, 1)
                for a in range(2):
                    c, w = divmod(n - 3 - 2 * a, NW)
                    if w == 0 and 0 <= c < NC:
                        scale_rows(c, a)

        @block.scalar
        def _(act):
            act.wait_ge(p_wce, 1)
            nc.scalar.activation(wce[:, :], fp[:, 0:P], ACT.Copy).then_inc(a_wce, 1)
            act.wait_ge(p_gram, 1)
            act.wait_ge(fill_ok, 5)
            for h in range(2):
                half = slice(D * h, D * h + D)
                nc.scalar.activation(gram[half, half], fp[half, P:P + D], ACT.Copy, scale=1.0 / E).then_inc(a_gram, 1)
            act.wait_ge(p_sw, 1)
            nc.scalar.activation(sw[SHIFT_ROWS, 0, :], up[0][SHIFT_ROWS, 0:PROJ], ACT.Copy).then_inc(a_sw, 1)
            centred = [0]

            def centre(dst, src, scratch, total):
                at = centred[0]
                nc.scalar.activation(scratch, src, ACT.Copy, accum_out=total[:, 0:1]).then_inc(wlc_ok, 1)
                act.wait_ge(wlc_ok, at + 1)
                nc.scalar.mul(total[:, 1:2], total[:, 0:1], -1.0 / MAXD).then_inc(wlc_ok, 1)
                act.wait_ge(wlc_ok, at + 2)
                nc.scalar.activation(dst, src, ACT.Identity, bias=total[:, 1:2]).then_inc(wlc_ok, 1)
                act.wait_ge(wlc_ok, at + 3)
                centred[0] += 3

            act.wait_ge(p_x, 1)
            nc.scalar.activation(xsq[:, :], vp[0], ACT.Square).then_inc(a_xsq, 1)

            def std_of_rows(c, a):
                t0, t1 = GROUP[a]
                act.wait_ge(var_ok, 2 * c + a + 1)
                nc.scalar.activation(std[:, t0:t1], var[:, t0:t1], ACT.Sqrt, bias=eps[:, 0:1]).then_inc(std_ok, 1)

            for n in range(SLOTS):
                c, w = divmod(n, NW)
                m = n - LG - 1
                if 0 <= m < N:
                    act.wait_ge(g_done, m + 1)
                    k = m // (2 * NW)
                    if m % (2 * NW) == 0 and k >= 2:
                        act.wait_ge(zt_ok, 2 * (k - 1))
                    g0 = NG * (m % (2 * NW))
                    nc.scalar.activation(
                        zs[:, k % 2, g0:g0 + NG, :],
                        gp[:, 0:GPW].rearrange("p (g c) -> p g c", g=NG),
                        ACT.Copy).then_inc(g_copied, 1)
                k = block_at(n, 2)
                if k is not None:
                    act.wait_ge(zt_ok, 2 * k + 1)
                    nc.scalar.activation(zt[:, 2:C, PROJ:ROW], zt[:, 2:C, 0:WRAP], ACT.Copy).then_inc(zw_ok, 1)
                    act.wait_ge(zw_ok, 2 * k + 1)
                    at = 2 * ROW + 1
                    nc.scalar.activation(
                        zp[:, :, :],
                        ZT[:, at:at + (ROW + 1) * PROJ].rearrange("p (q r) -> p q r", q=PROJ)[:, :, 0:WRAP],
                        ACT.Copy).then_inc(zw_ok, 1)
                if c < NC:
                    act.wait_ge(et_t, n + 1)
                    k = block_at(n, 3)
                    if k is not None:
                        act.wait_ge(f5_t, k + 1)
                        nc.scalar.activation(zf[0:FEAT5, NQ, :], etp[0:FEAT5, 2, :], ACT.Copy).then_inc(f5_ok, 1)
                    p0, np_ = PAIRS[w][0], len(PAIRS[w])
                    nc.scalar.activation(et[:, p0:p0 + np_, :], etp[:, 0:np_, :], ACT.Copy).then_inc(et_c, 1)
                k = block_at(n, 3)
                if k is not None:
                    act.wait_ge(f_t, k + 1)
                    nc.scalar.activation(zf[:, 0:NQ, :], f_bank(k).rearrange("p (i b) -> p i b", i=NQ), ACT.Copy).then_inc(f_c, 1)
                    if c >= NC:
                        act.wait_ge(f5_t, k + 1)
                        nc.scalar.activation(zf[0:FEAT5, NQ, :], etp[0:FEAT5, 2, :], ACT.Copy).then_inc(f5_ok, 1)
                k = block_at(n, 6)
                if k is not None:
                    act.wait_ge(o_done, k + 1)
                    nc.scalar.activation(osq[:, :], f_bank(k), ACT.Square, accum_out=ost[:, 0:1]).then_inc(o_ss, 1)
                    act.wait_ge(o_ss, k + 1)
                    nc.scalar.activation(ost[:, 1:2], ost[:, 0:1], ACT.Sqrt, bias=eps[:, 0:1],
                                         scale=1.0 / MAXD).then_inc(o_sd, 1)
                m = n - LV - 1
                if 0 <= m < N:
                    act.wait_ge(ss_ok, m + 1)
                    nc.scalar.activation(sd[:, m % 2, :], ss[:, m % 2, :], ACT.Sqrt, bias=eps[:, 0:1],
                                         scale=1.0 / PROJ).then_inc(sd_ok, 1)
                k = block_at(n, 10)
                if k is not None:
                    act.wait_ge(m2_done, k + 1)
                    for i in range(2):
                        nc.scalar.activation(h2[:, i, :], f_bank(k)[:, i * BLK:(i + 1) * BLK], ACT.Relu,
                                             bias=b2_c[:, i:i + 1]).then_inc(h2_ok, 1)
                m = n - LC
                if 0 <= m < N:
                    act.wait_ge(u_done, m + 1)
                    for h in range(2):
                        nc.scalar.activation(u[HALVES[h], m % 2, h, :], up[m % 2][HALVES[h], 0:HP],
                                             ACT.Copy).then_inc(u_copied, 1)
                k = block_at(n, 9)
                if k is not None:
                    act.wait_ge(hs_ok, k + 1)
                    nc.scalar.activation(h1[:, :, :], h1s[:, :, :], ACT.Relu).then_inc(h1_ok, 1)
                for a in range(2):
                    cc, ww = divmod(n - 3 - 2 * a, NW)
                    if ww == 0 and 0 <= cc < NC:
                        std_of_rows(cc, a)
                k = block_at(n, 10)
                if k is not None:
                    act.wait_ge(m3_done, k + 1)
                    nc.scalar.activation(y_sb[:, k * BLK:(k + 1) * BLK], f_bank(k)[0:1, 0:BLK], ACT.Copy).then_inc(y_ok, 1)
                k = block_at(n, 7)
                if k is not None:
                    if k == 0:
                        act.wait_ge(ld_top, 16 * 6)
                    act.wait_ge(z_t, k + 1)
                    for i in range(3):
                        nc.scalar.activation(zn[:, i, :], f_bank(k)[:, i * BLK:(i + 1) * BLK], ACT.Identity,
                                             bias=bl_c[:, i:i + 1], scale=gl_c[:, i:i + 1]).then_inc(z_c, 1)
                if w == 0 and 0 < c <= NC:
                    if c == 1:
                        act.wait_ge(xt_ok, 1)
                    k, h = divmod(c - 1, 2)
                    nc.scalar.activation(
                        T[:, (c - 1) % 2, :, 0].rearrange("p (g j) -> p g j", j=4),
                        xt[:, k * BLK:(k + 1) * BLK].rearrange("p (j g) -> p g j", j=4)[:, 16 * h:16 * h + 16, :],
                        ACT.Copy).then_inc(x_in, 1)
                if 1 <= n < 5:
                    i = n - 1
                    act.wait_ge(hd_done, n)
                    nc.scalar.activation(h1d[:, i, :], hd_bank[i], ACT.Identity, bias=b1_c[:, i:i + 1]).then_inc(hd_ok, 1)
                if n == 0:
                    act.wait_ge(p_xv, 1)
                    act.wait_ge(fill_ok, 3)
                    nc.scalar.activation(xsd[:, :], vp[1], ACT.Sqrt, bias=eps[:, 0:1]).then_inc(a_xsd, 1)
                if n == 6:
                    act.wait_ge(p_s, 1)
                    nc.scalar.activation(sumx[:, :], fp[:, 0:NK], ACT.Copy).then_inc(a_s, 1)
                if n in WL_SLOTS[:NQ]:
                    i = WL_SLOTS.index(n)
                    if i == 0:
                        act.wait_ge(ld_wl, 80)
                    centre(wlc[:, i, :], wl_sb[:, i, :], wlm[:, i, :], lsum[:, 2 * i:2 * i + 2])
                if n in WLM_SLOTS:
                    i = WLM_SLOTS.index(n)
                    act.wait_ge(cf_ok, 1)
                    nc.scalar.activation(wlm[:, i, :], wlc[:, i, :], ACT.Copy, scale=cf[:, 0, i:i + 1]).then_inc(wl_ok, 1)
                if n == WL_SLOTS[NQ]:
                    centre(wlxc[:, :], wlx_sb[:, :], wl5[0:PROJ, :], lsum[0:PROJ, 8:10])
                if n == W5_SLOT + NQ:
                    act.wait_ge(p_w5, 1)
                    nc.scalar.activation(wl5[:, :], fp[0:FEAT5, :], ACT.Copy).then_inc(a_w5, 1)
                k = block_at(n, 6)
                if k is not None:
                    act.wait_ge(o_r, k + 1)
                    nc.scalar.activation(on[:, :], f_bank(k)[:, 0:USED], ACT.Copy, scale=ost[:, 2:3]).then_inc(on_ok, 1)
                m = n - LV
                if 0 <= m < N:
                    act.wait_ge(v_done, m + 1)
                    if m >= 2:
                        act.wait_ge(ss_ok, m - 1)
                    nc.scalar.activation(vsq[:, m % 2, :], vp[m % 2], ACT.Square).then_inc(sq_ok, 1)

        @block.tensor
        def _(pe):
            def keep_clock(bank, times):
                for _ in range(times):
                    nc.tensor.matmul(bank, bs3[:, :], shift_rows, start=True, stop=True)

            pe.wait_ge(ld_const, 16)
            pe.wait_ge(wc_ok, 1)
            nc.tensor.transpose(fp[:, 0:P], wc[:, :], ident).then_inc(p_wce, 1)
            pe.wait_ge(a_wce, 1)
            nc.tensor.matmul(fp[:, P:P + D], wce[:, :], wce[:, 0:D], start=True, stop=True).then_inc(p_gram, 1)
            pe.wait_ge(mix_ok, 1)
            pe.wait_ge(fill_ok, 3)
            nc.tensor.matmul(up[0][:, 0:PROJ], ones_1[0:N_TBL, :], wsic[0:N_TBL, 0, :],
                             start=True, stop=True).then_inc(p_sw, 1)
            pe.wait_ge(a_gram, 2)
            pe.wait_ge(a_sw, 1)

            pe.wait_ge(wd_ok, 1)
            for i in range(2):
                last = nc.tensor.matmul(vp[0], wdc[:, i, :], dn[:, i, :], start=(i == 0), stop=(i == 1))
            last.then_inc(p_x, 1)
            def out_tile(k, i):
                nc.tensor.matmul(f_bank(k), zf[:, i, :], wlm[:, i, :], start=(i == 0), stop=False)

            def first_layer(k, i):
                for kk in range(3):
                    last = nc.tensor.matmul(f_bank(k)[:, i * BLK:(i + 1) * BLK], w1_sb[:, kk, i * P:(i + 1) * P],
                                            zn[:, kk, :], start=(kk == 0), stop=(kk == 2))
                return last

            def second_layer(k, i):
                for kk in range(4):
                    last = nc.tensor.matmul(f_bank(k)[:, i * BLK:(i + 1) * BLK], w2_sb[:, kk, i * P:(i + 1) * P],
                                            h1[:, kk, :], start=(kk == 0), stop=(kk == 3))
                return last

            for n in range(SLOTS):
                c, w = divmod(n, NW)
                if n == N + 1:
                    pe.wait_ge(qe_done, 2 * NC)
                k = block_at(n, 3)
                if k is not None:
                    pe.wait_ge(et_c, min(n, N))
                    pe.wait_ge(zt_ok, 2 * k + 2)
                    nc.tensor.transpose(etp[0:FEAT5, 2, :], ZT[:, 0:FEAT5], ident).then_inc(f5_t, 1)
                if c < NC:
                    for p in PAIRS[w]:
                        t0 = min(2 * p, TILES - 2)
                        pe.wait_ge(gath[c % NBUF][p], (c // NBUF + 1) * (32 if 2 * p + 1 < TILES else 16))
                        if n and p == PAIRS[w][0]:
                            pe.wait_ge(et_c, n)
                        last = nc.tensor.transpose(etp[:, p - PAIRS[w][0], :],
                                                   emb[:, c % NBUF, t0:t0 + 2, :].rearrange("p t d -> p (t d)"),
                                                   ident)
                    last.then_inc(et_t, 1)
                k = block_at(n, 7)
                if k is not None:
                    if k == NK - 1:
                        keep_clock(qp_bank, 3)
                    pe.wait_ge(on_ok, k + 1)
                    for i in range(3):
                        last = nc.tensor.transpose(f_bank(k)[:, i * BLK:(i + 1) * BLK], on[:, i * BLK:(i + 1) * BLK], ident)
                    last.then_inc(z_t, 1)
                k = block_at(n, 3)
                if k is not None:
                    pe.wait_ge(zw_ok, 2 * k + 2)
                    if k == 0:
                        pe.wait_ge(a_w5, 1)
                        pe.wait_ge(wl_ok, NQ)
                    if 1 <= k < NK - 1:
                        pe.wait_ge(y_ok, k)
                    for i in range(NQ):
                        src = zp[:, QT * i:QT * (i + 1), :].rearrange("p q r -> p (q r)")
                        last = nc.tensor.transpose(f_bank(k)[:, i * BLK:(i + 1) * BLK], src, ident)
                    last.then_inc(f_t, 1)
                k = block_at(n, 10)
                if k is not None:
                    second_layer(k, 1).then_inc(m2_done, 1)
                k = block_at(n, 4)
                if k is not None:
                    out_tile(k, 1)
                k = block_at(n, 5)
                if k is not None:
                    out_tile(k, 3)
                k = block_at(n, 8)
                if k is not None:
                    first_layer(k, 1)
                if 1 <= n <= N:
                    cq, wq = divmod(n - 1, NW)
                    pe.wait_ge(et_c, n)
                    for p in PAIRS[wq]:
                        a = int(2 * p >= GROUP[1][0])
                        if 2 * p == GROUP[a][0] and 2 * cq + a:
                            pe.wait_ge(qe_done, 2 * cq + a)
                        at, lone = 2 * p - GROUP[a][0], 2 * p + 1 == TILES
                        last = nc.tensor.matmul(
                            qp[:, at:at + 2 - lone, :], et[:, p, :], gram[:, D * lone:], start=True, stop=True)
                        if p == PAIRS[1][-1] or lone:
                            last.then_inc(q_done, 1)
                m = n - LC
                if 0 <= m < N:
                    cm, wm = divmod(m, NW)
                    pe.wait_ge(es_ok, 2 * cm + (2 if wm >= 2 else 1))
                    if m == 0:
                        pe.wait_ge(mix_ok, 2)
                    if m >= 2:
                        pe.wait_ge(u2_ok, 2 * (m - 1))
                    halves = [pieces(2 * wm), pieces(2 * wm + 1)]
                    for i in range(max(map(len, halves))):
                        for part, tiles in zip(HALVES, halves):
                            if i < len(tiles):
                                t, s0, ns, at = tiles[i]
                                last = nc.tensor.matmul(
                                    up[m % 2][part, PROJ * s0:PROJ * (s0 + ns)], es[:, cm % 2, t, :],
                                    mix[:, t, at:at + ns, :].rearrange("p b q -> p (b q)"),
                                    start=(i == 0), stop=(i == len(tiles) - 1), skip_group_check=True)
                    last.then_inc(u_done, 1)
                m = n - LV
                if 0 <= m < N:
                    if m == 0:
                        pe.wait_ge(wc_ok, 3)
                        pe.wait_ge(xt_ok, 1)
                    if m >= 2:
                        pe.wait_ge(t_ok, m - 1)
                    keep_clock(vp[m % 2], 0 if n < LIGHT else 0 if n > N else 0)
                    nc.tensor.matmul(vp[m % 2], bs3[:, :], shift_rows, start=True, stop=False)
                    pe.wait_ge(u2_ok, 2 * (m + 1))
                    for i, (w, x) in enumerate((
                            (wg_hi[:, :], u[:, m % 2, :, :].rearrange("p h c -> p (h c)")),
                            (wg_lo[:, :], u[:, m % 2, :, :].rearrange("p h c -> p (h c)")))):
                        last = nc.tensor.matmul(vp[m % 2], w, x, start=False, stop=(i == 1))
                    last.then_inc(v_done, 1)
                m = n - LG
                if 0 <= m < N:
                    cm, wm = divmod(m, NW)
                    if n > N + 5:
                        keep_clock(qp_bank, 3)
                    pe.wait_ge(t_ok, m + 1)
                    pe.wait_ge(x_in, cm + 1)
                    if m == 0:
                        pe.wait_ge(fill_ok, 4)
                    if m >= 1:
                        pe.wait_ge(g_copied, m)
                    for g in range(NG):
                        for j in range(4):
                            s = WIN * wm + 4 * g + j
                            at = C * g
                            last = nc.tensor.matmul(gp[32 * j:32 * j + 32, at:at + C], T[:, cm % 2, s, 2:C],
                                                    T[:, cm % 2, s, :], start=True, stop=True)
                    last.then_inc(g_done, 1)
                if 1 <= n < 5:
                    if n == 1:
                        pe.wait_ge(ld_x, 32)
                        pe.wait_ge(ld_dense, 32)
                    for i in range(2):
                        last = nc.tensor.matmul(hd_bank[n - 1], w1_sb[:, 3 + i, (n - 1) * P:n * P], dn[:, i, :],
                                                start=(i == 0), stop=(i == 1))
                    last.then_inc(hd_done, 1)
                if n == 0:
                    pe.wait_ge(a_xsq, 1)
                    nc.tensor.matmul(vp[1], ones_e[:, :], xsq[:, :], start=True, stop=True).then_inc(p_xv, 1)
                if n == 5:
                    pe.wait_ge(xt_ok, 1)
                    pe.wait_ge(hd_ok, 4)
                    for k in range(NK):
                        last = nc.tensor.matmul(fp[:, k:k + 1], xt[:, k * BLK:(k + 1) * BLK], ones_1[:, 0:1],
                                                start=True, stop=True)
                    last.then_inc(p_s, 1)
                if W5_SLOT <= n < W5_SLOT + NQ:
                    i = n - W5_SLOT
                    if i == 0:
                        pe.wait_ge(a_s, 1)
                        pe.wait_ge(m_ok, 1)
                        pe.wait_ge(wlc_ok, 3 * (NQ + 1))
                    nc.tensor.matmul(fp[0:FEAT5, :], mm[:, i, :], wlc[:, i, :], start=(i == 0), stop=False)
                if n == W5_SLOT + NQ:
                    nc.tensor.matmul(fp[0:FEAT5, :], mmx[:, :], wlxc[:, :], start=False, stop=True).then_inc(p_w5, 1)
                k = block_at(n, 3)
                if k is not None:
                    pe.wait_ge(f_c, k + 1)
                    out_tile(k, 0)
                k = block_at(n, 4)
                if k is not None:
                    out_tile(k, 2)
                k = block_at(n, 5)
                if k is not None:
                    pe.wait_ge(f5_ok, k + 1)
                    nc.tensor.matmul(f_bank(k), zf[0:FEAT5, NQ, :], wl5[:, :], start=False, stop=True).then_inc(o_done, 1)
                k = block_at(n, 7)
                if k is not None:
                    if k == NK - 1:
                        keep_clock(qp_bank, 2)
                    pe.wait_ge(z_c, 3 * k + 3)
                    first_layer(k, 0)
                k = block_at(n, 8)
                if k is not None:
                    first_layer(k, 2)
                    first_layer(k, 3).then_inc(m1_done, 1)
                k = block_at(n, 9)
                if k is not None:
                    if k == NK - 1:
                        keep_clock(qp_bank, 2)
                    pe.wait_ge(h1_ok, k + 1)
                    second_layer(k, 0)
                k = block_at(n, 10)
                if k is not None:
                    if k == NK - 1:
                        keep_clock(qp_bank, 1)
                    pe.wait_ge(h2_ok, 2 * k + 2)
                    for kk in range(2):
                        last = nc.tensor.matmul(f_bank(k)[0:1, 0:BLK], w3_c[:, kk:kk + 1], h2[:, kk, :],
                                                start=(kk == 0), stop=(kk == 1))
                    last.then_inc(m3_done, 1)


def layouts(inputs):
    f = {k: np.asarray(v) for k, v in inputs.items()}
    a = {}
    a["tables"] = np.concatenate([f[f"tbl_{i}"] for i in range(N_TBL)], 0)
    s = np.arange(B)
    order = s // BLK * BLK + 32 * (s % 4) + s % BLK // 4
    a["ids"] = f["ids"][order].reshape(NC * TILES, P).T
    starts = np.concatenate([[0], np.cumsum(VOCAB)[:-1]]).astype(a["ids"].dtype)
    a["base"] = np.tile(starts, B).reshape(NC * TILES, P).T
    rows = np.arange(TILES * P).reshape(TILES, P)
    mask = (rows // N_TBL - (rows[:, :1] // N_TBL))[:, :, None] == np.arange(TOUCH)
    q, k = np.meshgrid(np.arange(PROJ), 1 + np.arange(WRAP), indexing="ij")
    p = (q + k) % PROJ
    used = ~((k == WRAP) & (q >= WRAP))
    q, p, used = (x.reshape(NQ, P) for x in (q, p, used))
    hot = lambda x: (ROW + x[:, :, None] == np.arange(FEAT5)).transpose(1, 0, 2).reshape(P, -1)
    pick = np.zeros((P, 4))
    pick[SHIFT_ROWS] = [[1, 0, 1, 0], [1, 0, 0, 1], [0, 1, 1, 0]]
    a["consts"] = np.concatenate(
        [np.eye(P), mask.transpose(1, 0, 2).reshape(P, -1), hot(q), hot(p), pick], 1).astype(np.float32)
    a["wst"] = np.concatenate([f["L0_rec_Ws"].T] * 2, 0)
    a["wsi_rows"] = f["L0_rec_Wsi"].T[rows % N_TBL].transpose(1, 0, 2)
    a["gs"], a["bs"] = f["L0_rec_gs"][None], f["L0_rec_bs"][None]
    gsi, bsi = f["L0_rec_gsi"], f["L0_rec_bsi"]
    a["gsi_pairs"] = np.stack([gsi[q], gsi[p], bsi[q], bsi[p]]).transpose(2, 0, 1)
    a["gsi"], a["bsi"] = gsi[:, None], bsi[:, None]
    wl = f["L0_rec_Wl"].T
    i, j = np.maximum(p, q) + 1, np.minimum(p, q) + 1
    a["wlt"] = np.where(used[:, :, None], wl[i * (i - 1) // 2 + j], np.float32(0)).transpose(1, 0, 2)
    i = np.arange(PROJ) + 1
    a["wlx"] = wl[i * (i - 1) // 2]
    tiles = lambda x: x.reshape(-1, P, x.shape[-1]).transpose(1, 0, 2)
    cols = lambda x: x.reshape(-1, P).T
    a["dense_t"] = tiles(f["r_dense_t"].T)
    a["wdt"] = tiles(f["L0_rec_Wd"].T)
    a["gd"], a["bd"] = cols(f["L0_rec_gd"]), cols(f["L0_rec_bd"])
    a["gl"], a["bl"] = cols(f["L0_rec_gl"][:USED]), cols(f["L0_rec_bl"][:USED])
    w1 = f["W_top1"]
    a["w1"] = tiles(np.concatenate([w1[:USED], w1[MAXD:]], 0))
    a["b1"] = cols(f["b_top1"])
    a["w2"] = tiles(f["W_top2"])
    a["b2"] = cols(f["b_top2"])
    a["w3"] = cols(f["W_top3"][:, 0])
    return {"in_" + n: np.ascontiguousarray(x) for n, x in a.items()}


def kernel(**inputs):
    import concourse.bacc as bacc
    from concourse.bass_utils import run_bass_kernel_spmd

    arrays = layouts(inputs)
    nc = bacc.Bacc("TRN2", target_bir_lowering=False, num_devices=1)
    args = []
    for name, x in arrays.items():
        ap = nc.dram_tensor(name, x.shape, mybir.dt.from_np(x.dtype), kind="ExternalInput").ap()
        args.append(ap.bitcast(U32) if x.dtype.kind == "i" else ap)
    out = nc.dram_tensor("out_0", (1, B), F32, kind="ExternalOutput").ap()
    tower(nc, *args, out)
    got = run_bass_kernel_spmd(nc, [arrays], core_ids=[0])
    return got.results[0]["out_0"].reshape(B, 1)
```
